# Optimizing a Trainium2 kernel written in Bass

```python
import numpy as np
import jax
import jax.numpy as jnp

def _softmax(x, axis=-1):
    return jax.nn.softmax(x, axis=axis)

def _gelu(x):
    return jax.nn.gelu(x, approximate=True)

def _silu(x):
    return jax.nn.silu(x)

def _sigmoid(x):
    return jax.nn.sigmoid(x)

def _layernorm(x, axis=-1, eps=1e-05):
    m = jnp.mean(x, axis=axis, keepdims=True)
    v = jnp.var(x, axis=axis, keepdims=True)
    return (x - m) / jnp.sqrt(v + eps)

def _scatter_add(tgt, idx, src, axis=0):
    return tgt.at[idx].add(src)

def _segment_sum(src, seg, n):
    return jax.ops.segment_sum(src, seg, n)
kernel_name = 'mk_xattn_ffn_d2_seqx_r4_7e9017'

def setup_inputs(seed: int=0):
    np.random.seed(seed)
    _w = jnp.asarray

    def _rec_inputs():
        import jax
        import jax.numpy as jnp
        _rk = jax.random.key(seed)
        x = -0.0002928 + 1 * jax.random.normal(jax.random.fold_in(_rk, 1), (16, 512, 256), jnp.float32)
        _lenS = 512 - jax.random.randint(jax.random.fold_in(_rk, 7), (16,), 0, max(1, 512 // 4) + 1, jnp.int32)
        _lenS2 = 64 - jax.random.randint(jax.random.fold_in(_rk, 8), (16,), 0, max(1, 64 // 4) + 1, jnp.int32)
        _ctx_1024P = jax.random.normal(jax.random.fold_in(_rk, 11), (16, 16, 256), jnp.float32)
        _ctx_1024c = jax.random.dirichlet(jax.random.fold_in(_rk, 511), 0.3 * jnp.ones((16,), jnp.float32), (16, 64))
        _ctx_1024t = jnp.einsum('bsk,bkd->bsd', _ctx_1024c, _ctx_1024P)
        _ctx_1024t = _ctx_1024t * jax.lax.rsqrt(jnp.mean(jnp.square(_ctx_1024t)) + 1e-12) * 0.953939
        ctx_1024 = -1.39393e-06 + 0.999914 * (_ctx_1024t + 0.3 * jax.random.normal(jax.random.fold_in(_rk, 611), (16, 64, 256), jnp.float32))
        _validS = jnp.arange(512)[None, :] < _lenS[:, None]
        _validS2 = jnp.arange(64)[None, :] < _lenS2[:, None]
        _causal = jnp.tril(jnp.ones((512, 512), dtype=bool))
        mask_Bx1xSxS2_fk0 = jnp.where(jnp.broadcast_to(_validS2[:, None, None, :], (16, 1, 512, 64)), 0.0, 1.0).astype(jnp.float32)
        mask_Bx1xSxS2_ik1 = jnp.where(jnp.broadcast_to(_validS2[:, None, None, :], (16, 1, 512, 64)), 1, 0).astype(jnp.int32)
        return (x, ctx_1024, mask_Bx1xSxS2_fk0, mask_Bx1xSxS2_ik1)
    x, ctx_1024, mask_Bx1xSxS2_fk0, mask_Bx1xSxS2_ik1 = _rec_inputs()

    def _L0_xattn_setup():
        import jax, jax.numpy as jnp
        import numpy as np
        B, S, D, H = (2, 512, 256, 16)
        K = D // H

        def _split_heads(x):
            b, s, _ = x.shape
            return x.reshape(b, s, H, K).transpose(0, 2, 1, 3)
        key = jax.random.key(seed)
        ks = jax.random.split(key, 8)
        scale = 1.0 / np.sqrt(D)
        dec = jax.random.normal(ks[0], (B, S, D), dtype=jnp.float32)
        enc = jax.random.normal(ks[1], (B, S, D), dtype=jnp.float32)
        mask = jnp.broadcast_to(jnp.tril(jnp.ones((S, S), jnp.float32))[None, None], (B, 1, S, S))
        return {'decoder_input': dec, 'encoder_output': enc, 'mask': mask, 'Wq': jax.random.normal(ks[2], (D, D), jnp.float32) * scale, 'bq': jnp.zeros((D,), jnp.float32), 'Wk': jax.random.normal(ks[3], (D, D), jnp.float32) * scale, 'bk': jnp.zeros((D,), jnp.float32), 'Wv': jax.random.normal(ks[4], (D, D), jnp.float32) * scale, 'bv': jnp.zeros((D,), jnp.float32), 'Wo': jax.random.normal(ks[5], (D, D), jnp.float32) * scale, 'bo': jnp.zeros((D,), jnp.float32)}
    _L0_xattn_all = _L0_xattn_setup()
    _L0_xattn_in = {k: v for k, v in _L0_xattn_all.items() if k in ('Wq', 'bq', 'Wk', 'bk', 'Wv', 'bv', 'Wo', 'bo')}
    del _L0_xattn_all

    def _L0_ffn_setup():
        import jax, jax.numpy as jnp
        import numpy as np
        BLOCK = 32
        W_BITS = 4
        ACT_BITS = 16

        def act_qdq(x):
            qmax = 2.0 ** (ACT_BITS - 1) - 1.0
            scale = jnp.maximum(jnp.max(jnp.abs(x)) / qmax, 1e-12)
            return jnp.clip(jnp.round(x / scale), -qmax - 1.0, qmax) * scale

        def fixed_qdq_u16(x):
            scale = 1.0 / 65536.0
            return jnp.clip(jnp.round(x / scale), 0.0, 65535.0) * scale

        def lpbq_dequant(w):
            O, I = w.shape
            qmax = 2.0 ** (W_BITS - 1) - 1.0
            wb = w.reshape(O, I // BLOCK, BLOCK)
            s = jnp.maximum(jnp.max(jnp.abs(wb), axis=-1, keepdims=True) / qmax, 1e-12)
            wq = jnp.clip(jnp.round(wb / s), -qmax - 1.0, qmax) * s
            return wq.reshape(O, I)
        key = jax.random.key(seed)
        k1, k2, k3, k4 = jax.random.split(key, 4)
        B, S, H, I = (2, 1024, 256, 768)
        x = jax.random.normal(k1, (B, S, H), jnp.float32)
        w_gate = jax.random.normal(k2, (I, H), jnp.float32) * 0.02
        w_up = jax.random.normal(k3, (I, H), jnp.float32) * 0.02
        w_down = jax.random.normal(k4, (H, I), jnp.float32) * 0.02
        return {'x': x, 'w_gate': w_gate, 'w_up': w_up, 'w_down': w_down}
    _L0_ffn_all = _L0_ffn_setup()
    _L0_ffn_in = {k: v for k, v in _L0_ffn_all.items() if k in ('w_gate', 'w_up', 'w_down')}
    del _L0_ffn_all

    def _L1_xattn_setup():
        import jax, jax.numpy as jnp
        import numpy as np
        EMBED_SIZE = 256
        HEADS = 16
        HEAD_DIM = EMBED_SIZE // HEADS
        N, L = (2, 512)
        key = jax.random.key(seed)
        ks = jax.random.split(key, 6)
        values = jax.random.normal(ks[0], (N, L, EMBED_SIZE), dtype=jnp.float32)
        keys_t = jax.random.normal(ks[1], (N, L, EMBED_SIZE), dtype=jnp.float32)
        query = jax.random.normal(ks[2], (N, L, EMBED_SIZE), dtype=jnp.float32)
        mask = jax.random.randint(ks[3], (N, 1, L, L), 0, 2, dtype=jnp.int32)
        Wo = jax.random.normal(ks[4], (EMBED_SIZE, EMBED_SIZE), dtype=jnp.float32) * EMBED_SIZE ** (-0.5)
        bo = jax.random.normal(ks[5], (EMBED_SIZE,), dtype=jnp.float32) * 0.01
        return {'values': values, 'keys': keys_t, 'query': query, 'mask': mask, 'Wo': Wo, 'bo': bo}
    _L1_xattn_all = _L1_xattn_setup()
    _L1_xattn_in = {k: v for k, v in _L1_xattn_all.items() if k in ('Wo', 'bo')}
    del _L1_xattn_all

    def _L1_ffn_setup():
        import jax, jax.numpy as jnp
        import numpy as np
        HIDDEN = 256
        INTER = 128
        N_EXPERTS = 16
        N_GROUP = 4
        TOPK_GROUP = 2
        TOP_K = 4
        SCALING = 2.5

        def _gate(x_flat, gate_w, e_bias):
            logits = x_flat @ gate_w.T
            scores = jax.nn.sigmoid(logits)
            scores_for_choice = scores + e_bias[None, :]
            T = x_flat.shape[0]
            per_group = N_EXPERTS // N_GROUP
            grouped = scores_for_choice.reshape(T, N_GROUP, per_group)
            top2, _ = jax.lax.top_k(grouped, 2)
            group_scores = top2.sum(-1)
            _, group_idx = jax.lax.top_k(group_scores, TOPK_GROUP)
            group_mask = jax.nn.one_hot(group_idx, N_GROUP, dtype=jnp.float32).sum(1) > 0
            score_mask = jnp.repeat(group_mask, per_group, axis=-1)
            tmp_scores = jnp.where(score_mask, scores_for_choice, 0.0)
            _, topk_idx = jax.lax.top_k(tmp_scores, TOP_K)
            topk_weight = jnp.take_along_axis(scores, topk_idx, axis=1)
            topk_weight = topk_weight / (topk_weight.sum(-1, keepdims=True) + 1e-20)
            topk_weight = topk_weight * SCALING
            return (topk_idx, topk_weight)
        key = jax.random.key(seed)
        ks = jax.random.split(key, 8)
        B, S = (2, 512)
        hidden_states = jax.random.normal(ks[0], (B, S, HIDDEN), dtype=jnp.float32)
        gate_w = jax.random.normal(ks[1], (N_EXPERTS, HIDDEN), dtype=jnp.float32) * 0.02
        e_bias = jnp.zeros((N_EXPERTS,), dtype=jnp.float32)
        gate_proj = jax.random.normal(ks[2], (N_EXPERTS, INTER, HIDDEN), dtype=jnp.float32) * 0.02
        up_proj = jax.random.normal(ks[3], (N_EXPERTS, INTER, HIDDEN), dtype=jnp.float32) * 0.02
        down_proj = jax.random.normal(ks[4], (N_EXPERTS, HIDDEN, INTER), dtype=jnp.float32) * 0.02
        shared_gate_w = jax.random.normal(ks[5], (INTER, HIDDEN), dtype=jnp.float32) * 0.02
        shared_up_w = jax.random.normal(ks[6], (INTER, HIDDEN), dtype=jnp.float32) * 0.02
        shared_down_w = jax.random.normal(ks[7], (HIDDEN, INTER), dtype=jnp.float32) * 0.02
        return {'hidden_states': hidden_states, 'gate_w': gate_w, 'e_bias': e_bias, 'gate_proj': gate_proj, 'up_proj': up_proj, 'down_proj': down_proj, 'shared_gate_w': shared_gate_w, 'shared_up_w': shared_up_w, 'shared_down_w': shared_down_w}
    _L1_ffn_all = _L1_ffn_setup()
    _L1_ffn_in = {k: v for k, v in _L1_ffn_all.items() if k in ('gate_w', 'e_bias', 'gate_proj', 'up_proj', 'down_proj', 'shared_gate_w', 'shared_up_w', 'shared_down_w')}
    del _L1_ffn_all
    return {'x': x, 'ctx_1024': ctx_1024, 'mask_Bx1xSxS2_fk0': mask_Bx1xSxS2_fk0, 'mask_Bx1xSxS2_ik1': mask_Bx1xSxS2_ik1, 'L0_xattn_Wq': _L0_xattn_in['Wq'], 'L0_xattn_bq': _L0_xattn_in['bq'], 'L0_xattn_Wk': _L0_xattn_in['Wk'], 'L0_xattn_bk': _L0_xattn_in['bk'], 'L0_xattn_Wv': _L0_xattn_in['Wv'], 'L0_xattn_bv': _L0_xattn_in['bv'], 'L0_xattn_Wo': _L0_xattn_in['Wo'], 'L0_xattn_bo': _L0_xattn_in['bo'], 'L0_ffn_w_gate': _L0_ffn_in['w_gate'], 'L0_ffn_w_up': _L0_ffn_in['w_up'], 'L0_ffn_w_down': _L0_ffn_in['w_down'], 'L1_xattn_Wo': _L1_xattn_in['Wo'], 'L1_xattn_bo': _L1_xattn_in['bo'], 'L1_ffn_gate_w': _L1_ffn_in['gate_w'], 'L1_ffn_e_bias': _L1_ffn_in['e_bias'], 'L1_ffn_gate_proj': _L1_ffn_in['gate_proj'], 'L1_ffn_up_proj': _L1_ffn_in['up_proj'], 'L1_ffn_down_proj': _L1_ffn_in['down_proj'], 'L1_ffn_shared_gate_w': _L1_ffn_in['shared_gate_w'], 'L1_ffn_shared_up_w': _L1_ffn_in['shared_up_w'], 'L1_ffn_shared_down_w': _L1_ffn_in['shared_down_w']}

def reference(x, ctx_1024, mask_Bx1xSxS2_fk0, mask_Bx1xSxS2_ik1, L0_xattn_Wq, L0_xattn_bq, L0_xattn_Wk, L0_xattn_bk, L0_xattn_Wv, L0_xattn_bv, L0_xattn_Wo, L0_xattn_bo, L0_ffn_w_gate, L0_ffn_w_up, L0_ffn_w_down, L1_xattn_Wo, L1_xattn_bo, L1_ffn_gate_w, L1_ffn_e_bias, L1_ffn_gate_proj, L1_ffn_up_proj, L1_ffn_down_proj, L1_ffn_shared_gate_w, L1_ffn_shared_up_w, L1_ffn_shared_down_w):
    import jax
    import jax.numpy as jnp

    def _L0_xattn_ref(decoder_input, encoder_output, mask, Wq, bq, Wk, bk, Wv, bv, Wo, bo):
        import jax, jax.numpy as jnp
        import numpy as np
        B, S, D, H = (2, 512, 256, 16)
        K = D // H

        def _split_heads(x):
            b, s, _ = x.shape
            return x.reshape(b, s, H, K).transpose(0, 2, 1, 3)
        q = _split_heads(decoder_input @ Wq + bq)
        k = _split_heads(encoder_output @ Wk + bk)
        v = _split_heads(encoder_output @ Wv + bv)
        score = jnp.einsum('bhqd,bhkd->bhqk', q, k) / jnp.sqrt(jnp.float32(K))
        score = score * mask
        score = jnp.where(score == 0, jnp.float32(-1000000000.0), score)
        align = jax.nn.softmax(score, axis=-1)
        ctx = jnp.einsum('bhqk,bhkd->bhqd', align, v)
        ctx = ctx.transpose(0, 2, 1, 3).reshape(decoder_input.shape[0], -1, D)
        return ctx @ Wo + bo

    def _L0_ffn_ref(x, w_gate, w_up, w_down):
        import jax, jax.numpy as jnp
        import numpy as np
        BLOCK = 32
        W_BITS = 4
        ACT_BITS = 16

        def act_qdq(x):
            qmax = 2.0 ** (ACT_BITS - 1) - 1.0
            scale = jnp.maximum(jnp.max(jnp.abs(x)) / qmax, 1e-12)
            return jnp.clip(jnp.round(x / scale), -qmax - 1.0, qmax) * scale

        def fixed_qdq_u16(x):
            scale = 1.0 / 65536.0
            return jnp.clip(jnp.round(x / scale), 0.0, 65535.0) * scale

        def lpbq_dequant(w):
            O, I = w.shape
            qmax = 2.0 ** (W_BITS - 1) - 1.0
            wb = w.reshape(O, I // BLOCK, BLOCK)
            s = jnp.maximum(jnp.max(jnp.abs(wb), axis=-1, keepdims=True) / qmax, 1e-12)
            wq = jnp.clip(jnp.round(wb / s), -qmax - 1.0, qmax) * s
            return wq.reshape(O, I)
        x = act_qdq(x)
        up = act_qdq(x @ lpbq_dequant(w_up).T)
        gate = act_qdq(x @ lpbq_dequant(w_gate).T)
        sig = fixed_qdq_u16(jax.nn.sigmoid(gate))
        gate = act_qdq(gate * sig)
        o = act_qdq(gate * up)
        return o @ lpbq_dequant(w_down).T

    def _L1_xattn_ref(values, keys, query, mask, Wo, bo):
        import jax, jax.numpy as jnp
        import numpy as np
        EMBED_SIZE = 256
        HEADS = 16
        HEAD_DIM = EMBED_SIZE // HEADS
        N, L = (2, 512)
        n, q_len, _ = query.shape
        v = values.reshape(n, -1, HEADS, HEAD_DIM)
        k = keys.reshape(n, -1, HEADS, HEAD_DIM)
        q = query.reshape(n, q_len, HEADS, HEAD_DIM)
        energy = jnp.einsum('nqhd,nkhd->nhqk', q, k)
        energy = jnp.where(mask == 0, jnp.float32(-1e+20), energy)
        scale = jnp.float32(EMBED_SIZE) ** 0.5
        attn = jax.nn.softmax(energy / scale, axis=3)
        out = jnp.einsum('nhqk,nkhd->nqhd', attn, v).reshape(n, q_len, HEADS * HEAD_DIM)
        return out @ Wo.T + bo

    def _L1_ffn_ref(hidden_states, gate_w, e_bias, gate_proj, up_proj, down_proj, shared_gate_w, shared_up_w, shared_down_w):
        import jax, jax.numpy as jnp
        import numpy as np
        HIDDEN = 256
        INTER = 128
        N_EXPERTS = 16
        N_GROUP = 4
        TOPK_GROUP = 2
        TOP_K = 4
        SCALING = 2.5

        def _gate(x_flat, gate_w, e_bias):
            logits = x_flat @ gate_w.T
            scores = jax.nn.sigmoid(logits)
            scores_for_choice = scores + e_bias[None, :]
            T = x_flat.shape[0]
            per_group = N_EXPERTS // N_GROUP
            grouped = scores_for_choice.reshape(T, N_GROUP, per_group)
            top2, _ = jax.lax.top_k(grouped, 2)
            group_scores = top2.sum(-1)
            _, group_idx = jax.lax.top_k(group_scores, TOPK_GROUP)
            group_mask = jax.nn.one_hot(group_idx, N_GROUP, dtype=jnp.float32).sum(1) > 0
            score_mask = jnp.repeat(group_mask, per_group, axis=-1)
            tmp_scores = jnp.where(score_mask, scores_for_choice, 0.0)
            _, topk_idx = jax.lax.top_k(tmp_scores, TOP_K)
            topk_weight = jnp.take_along_axis(scores, topk_idx, axis=1)
            topk_weight = topk_weight / (topk_weight.sum(-1, keepdims=True) + 1e-20)
            topk_weight = topk_weight * SCALING
            return (topk_idx, topk_weight)
        B, S, H = hidden_states.shape
        x = hidden_states.reshape(-1, H)
        T = x.shape[0]
        topk_idx, topk_weight = _gate(x, gate_w, e_bias)
        g = jnp.einsum('th,eih->eti', x, gate_proj)
        u = jnp.einsum('th,eih->eti', x, up_proj)
        inter = jax.nn.silu(g) * u
        expert_out = jnp.einsum('eti,ehi->eth', inter, down_proj)
        sel = expert_out[topk_idx, jnp.arange(T)[:, None]]
        y = jnp.einsum('tkh,tk->th', sel, topk_weight)
        y = y.reshape(B, S, H)
        sg = hidden_states @ shared_gate_w.T
        su = hidden_states @ shared_up_w.T
        shared_out = jax.nn.silu(sg) * su @ shared_down_w.T
        return y + shared_out
    x = x + _L0_xattn_ref(_layernorm(x, axis=-1), ctx_1024, mask_Bx1xSxS2_fk0, L0_xattn_Wq, L0_xattn_bq, L0_xattn_Wk, L0_xattn_bk, L0_xattn_Wv, L0_xattn_bv, L0_xattn_Wo, L0_xattn_bo)
    x = x + _L0_ffn_ref(_layernorm(x, axis=-1), L0_ffn_w_gate, L0_ffn_w_up, L0_ffn_w_down)
    x = x + _L1_xattn_ref(ctx_1024, ctx_1024, _layernorm(x, axis=-1), mask_Bx1xSxS2_ik1, L1_xattn_Wo, L1_xattn_bo)
    x = x + _L1_ffn_ref(_layernorm(x, axis=-1), L1_ffn_gate_w, L1_ffn_e_bias, L1_ffn_gate_proj, L1_ffn_up_proj, L1_ffn_down_proj, L1_ffn_shared_gate_w, L1_ffn_shared_up_w, L1_ffn_shared_down_w)
    return x

_drawn_inputs = setup_inputs


def setup_inputs(seed=0):
    import zlib

    import numpy as np

    out = dict(_drawn_inputs(seed))
    spreads = {'L0_xattn_bq': (0.0, 0.322),
     'L0_xattn_bk': (0.0, 0.8),
     'L0_xattn_bv': (0.0, 0.1),
     'L0_xattn_bo': (0.0, 0.1),
     'L1_ffn_e_bias': (0.0, 0.793)}
    factors = {'L1_xattn_bo': 7.206,
     'L1_ffn_gate_w': 6.658,
     'L1_ffn_gate_proj': 5.093,
     'L1_ffn_up_proj': 5.049,
     'L1_ffn_down_proj': 5.039,
     'L1_ffn_shared_gate_w': 6.133,
     'L1_ffn_shared_up_w': 5.631,
     'L1_ffn_shared_down_w': 5.653}
    for name, (base, spread) in spreads.items():
        noise = np.random.default_rng([zlib.crc32(name.encode()), seed]).standard_normal(out[name].shape)
        drawn = base * np.exp(spread * noise) if base else spread * noise
        out[name] = jnp.asarray(drawn.astype(out[name].dtype))
    for name, factor in factors.items():
        out[name] = (out[name] * factor).astype(out[name].dtype)
    return out
```

```python
from contextlib import ExitStack

import concourse.bass as bass
from concourse import mybir

P = 128
F32, F16, BF16 = mybir.dt.float32, mybir.dt.float16, mybir.dt.bfloat16
I32, I16, U16 = mybir.dt.int32, mybir.dt.int16, mybir.dt.uint16
ALU, ACT, AX = mybir.AluOpType, mybir.ActivationFunctionType, mybir.AxisListType
RMAX = bass.bass_isa.ReduceOp.max

B, S, D = 16, 512, 256
KEYS, HEADS, HD = 64, 16, 16
NT = B * S // P
TPB = S // P
KC = D // P
HPP = P // HD
PAIRS = HEADS // 2
VC = HD + 1
FF = 768
NI = FF // P
QB = 32
NE, INTER = 16, 128
GROUPS, PER_GROUP, TOPK_GROUP, TOP_K, SCALING = 4, 4, 2, 4, 2.5
WS = 64.0
QMAX = 32767.0
EPS = 1e-5
PASSES = ((0, 0), (0, 1), (1, 0))


def bc(ap, axis, n):
    a = ap.unsqueeze(axis)
    shape = list(a.shape)
    shape[axis] = n
    return a.to_broadcast(shape)


class Tiles:

    def __init__(self, count, unroll, lead, depth):
        self.count, self.unroll, self.lead, self.depth = count, unroll, lead, depth

    def run(self, eng, step):
        for n in range(self.lead):
            step(n // self.unroll, n % self.unroll, lambda lag, n=n: 0 <= n - lag < self.count)
        with eng.Fori(self.lead // self.unroll, self.count // self.unroll) as r:
            for j in range(self.unroll):
                step(r, j, lambda lag: True)
        for n in range(self.count, self.count + self.depth):
            step(n // self.unroll, n % self.unroll, lambda lag, n=n: 0 <= n - lag < self.count)


def since(value, least=1):
    return not isinstance(value, int) or value >= least


def wait(eng, sem, value):
    if since(value):
        eng.wait_ge(sem, value)


class Chain:

    def __init__(self, eng, sem):
        self.eng, self.sem, self.n = eng, sem, 0

    def __call__(self, ins):
        self.n += 1
        ins.then_inc(self.sem, 1)
        self.eng.wait_ge(self.sem, self.n)


class Stage:
    cleared = []

    def __init__(self, nc, name):
        self.nc, self.name, self.ctx, self.sems = nc, name, ExitStack(), []

    def __enter__(self):
        self.ctx.__enter__()
        return self

    def __exit__(self, *a):
        for sem in self.sems:
            self.nc.gpsimd.sem_clear(sem)
        for sem in Stage.cleared:
            self.nc.release_semaphore(sem)
        Stage.cleared = self.sems
        return self.ctx.__exit__(*a)

    def sb(self, name, shape, dt):
        return self.ctx.enter_context(self.nc.sbuf_tensor(f"{self.name}_{name}", shape, dt))

    def sem(self, name):
        self.sems.append(self.nc.alloc_semaphore(f"{self.name}_{name}"))
        return self.sems[-1]


def constants(nc, g):
    with Stage(nc, "const") as st:
        zeroed = st.sem("zeroed")
        written = st.sem("written")
        with nc.Block() as block:
            @block.gpsimd
            def _(pool):
                nc.gpsimd.memset(g.ident32[:, :], 0.0).then_inc(zeroed, 1)
                nc.gpsimd.memset(g.head_mask[:, :, :], 1.0).then_inc(zeroed, 1)
                pool.wait_ge(zeroed, 2)
                nc.gpsimd.affine_select(out=g.ident32[:, :], in_=g.ident32[:, :], compare_op=ALU.not_equal,
                                        fill=1.0, base=0, pattern=[[-1, P]], channel_multiplier=1).then_inc(written, 1)
                nc.gpsimd.affine_select(out=g.head_mask[:, :, :], in_=g.head_mask[:, :, :], compare_op=ALU.is_ge,
                                        fill=0.0, base=0, pattern=[[-HD, HPP], [0, KEYS]],
                                        channel_multiplier=1).then_inc(written, 1)
                pool.wait_ge(written, 2)
                nc.gpsimd.affine_select(out=g.head_mask[:, :, :], in_=g.head_mask[:, :, :], compare_op=ALU.is_ge,
                                        fill=0.0, base=HD - 1, pattern=[[HD, HPP], [0, KEYS]],
                                        channel_multiplier=-1).then_inc(written, 1)

            @block.vector
            def _(dve):
                dve.wait_ge(written, 1)
                nc.vector.tensor_copy(g.ident16[:, :], g.ident32[:, :])
                nc.vector.tensor_copy(g.identb[:, :], g.ident32[:, :])


def finish_stats(nc, eng, g, side, sems):
    steps, var_ready, std_ready, done = sems
    if side == "act":
        eng.wait_ge(var_ready, 1)
        nc.scalar.activation(g.rstd[:, :], g.var[:, :], ACT.Sqrt).then_inc(std_ready, 1)
        return
    chain = Chain(eng, steps)
    even_m, even_v = g.stats[:, :, 1], g.stats[:, :, 2]
    odd_m, odd_v = g.stats[:, :, 4], g.stats[:, :, 5]
    chain(nc.vector.tensor_tensor(g.mean[:, :], even_m, odd_m, ALU.add))
    chain(nc.vector.tensor_scalar(g.mean[:, :], g.mean[:, :], 0.5, None, ALU.mult))
    chain(nc.vector.tensor_tensor(g.var[:, :], even_m, odd_m, ALU.subtract))
    chain(nc.vector.tensor_tensor(g.var[:, :], g.var[:, :], g.var[:, :], ALU.mult))
    chain(nc.vector.tensor_scalar(g.var[:, :], g.var[:, :], 0.25, EPS, ALU.mult, ALU.add))
    chain(nc.vector.tensor_tensor(g.rstd[:, :], even_v, odd_v, ALU.add))
    chain(nc.vector.tensor_scalar(g.rstd[:, :], g.rstd[:, :], 1.0 / D, None, ALU.mult))
    nc.vector.tensor_tensor(g.var[:, :], g.var[:, :], g.rstd[:, :], ALU.add).then_inc(var_ready, 1)
    eng.wait_ge(std_ready, 1)
    nc.vector.reciprocal(g.rstd[:, :], g.rstd[:, :]).then_inc(done, 1)


def attention_prep(nc, g, io, layer, kbd, vbd, wq, wo):
    with Stage(nc, f"prep{layer}") as st:
        ctx_t = st.sb("ctx_t", [P, KC, B * KEYS], F32)
        ctx_parts = st.sb("ctx_parts", [P, 2, KC, B * KEYS], F16)
        w_raw = st.sb("w_raw", [P, 4, KC, D], F32)
        loaded = {k: st.sem(f"loaded_{k}") for k in ("ctx", "w", "bias", "ctx_dup")}
        x_loaded = [st.sem(f"x_loaded{b}") for b in range(B if layer == 0 else 0)]
        split_hi, split_lo = st.sem("split_hi"), st.sem("split_lo")
        zeroed, ones_set = st.sem("zeroed"), st.sem("ones_set")
        k_product, k_hi, k_lo = st.sem("k_product"), st.sem("k_hi"), st.sem("k_lo")
        v_product, v_stored = st.sem("v_product"), st.sem("v_stored")
        stats_done = st.sem("stats_done")
        sems = (st.sem("stat_steps"), st.sem("var_ready"), st.sem("std_ready"), st.sem("rstd_ready"))
        ps = g.psum
        if layer == 0:
            wkv = st.sb("wkv", [P, 2, 2, KC, D], F16)
            v_bias = st.sb("v_bias", [P, PAIRS, HD], F32)
            key_bias = st.sb("key_bias", [P, KC], F32)
            k_parts = st.sb("k_parts", [P, 2, KC, B * KEYS], F16)
            names = ["L0_xattn_Wq", "L0_xattn_Wo", "L0_xattn_Wk", "L0_xattn_Wv"]
            targets = [wq, wo, wkv[:, 0], wkv[:, 1]]
        else:
            ctx_dup = st.sb("ctx_dup", [P, B, D], F32)
            k_parts = ctx_parts
            names = ["L1_xattn_WoT"]
            targets = [wo]
        NW = len(names)
        with nc.Block() as block:
            @block.sync
            def _(sp):
                sp.dma_start(ctx_t[:, :, :], io["ctx_T"].rearrange("(k p) n -> p k n", p=P)).then_inc(loaded["ctx"], 16)
                for n, name in enumerate(names):
                    sp.dma_start(w_raw[:, n], io[name].rearrange("(k p) n -> p k n", p=P)).then_inc(loaded["w"], 16)
                bo = io[f"L{layer}_xattn_bo"].rearrange("(a n) -> a n", a=1)
                sp.dma_start(g.out_bias[:, :], bo.to_broadcast([P, D])).then_inc(loaded["bias"], 16)
                if layer == 0:
                    sp.dma_start(g.q_bias[:, :], io["L0_xattn_bq"].rearrange("(k p) -> p k", p=P), allow_slow_non_contiguous=True).then_inc(loaded["bias"], 16)
                    sp.dma_start(key_bias[:, :], io["L0_xattn_bk"].rearrange("(k p) -> p k", p=P), allow_slow_non_contiguous=True).then_inc(loaded["bias"], 16)
                    bv = io["L0_xattn_bv"].rearrange("(p e d) -> e p d", e=2, d=HD)
                    for e in range(2):
                        sp.dma_start(v_bias[KEYS * e:KEYS * (e + 1)],
                                     bv[e:e + 1].to_broadcast([KEYS, PAIRS, HD])).then_inc(loaded["bias"], 16)
                    for b in range(B):
                        sp.dma_start(g.res[:, TPB * b:TPB * (b + 1), :],
                                     io["x"][b].rearrange("(t p) d -> p t d", p=P)).then_inc(x_loaded[b], 16)
                else:
                    for e in range(2):
                        sp.dma_start(ctx_dup[KEYS * e:KEYS * (e + 1)],
                                     io["ctx"].rearrange("b k d -> k b d")).then_inc(loaded["ctx_dup"], 16)
                sp.wait_ge(loaded["bias"], 16 * (5 if layer == 0 else 1))

            @block.gpsimd
            def _(pool):
                nc.gpsimd.memset(vbd[:, :, :, :], 0.0).then_inc(zeroed, 1)
                pool.wait_ge(zeroed, 1)
                for e in range(2):
                    col = e * VC + HD
                    nc.gpsimd.memset(vbd[KEYS * e:KEYS * (e + 1), :, :, col:col + 1], 1.0).then_inc(ones_set, 1)

            @block.scalar
            def _(act):
                act.wait_ge(loaded["ctx"], 16)
                nc.scalar.copy(ctx_parts[:, 0], ctx_t[:, :, :]).then_inc(split_hi, 1)
                for n in range(NW):
                    act.wait_ge(loaded["w"], 16 * NW)
                    nc.scalar.mul(targets[n][:, 0], w_raw[:, n], WS).then_inc(split_hi, 1)
                if layer == 0:
                    for h in range(KC):
                        for c in range(2):
                            n = 2 * h + c
                            act.wait_ge(k_product, n + 1)
                            act.wait_ge(loaded["bias"], 16 * 5)
                            nc.scalar.activation(k_parts[:, 0, h, 512 * c:512 * (c + 1)], ps[:, n], ACT.Identity,
                                                 bias=key_bias[:, h:h + 1], scale=1.0 / WS).then_inc(k_hi, 1)
                finish_stats(nc, act, g, "act", sems)

            @block.tensor
            def _(pe):
                if layer:
                    return
                pe.wait_ge(split_lo, 1 + NW)
                for h in range(KC):
                    for c in range(2):
                        for k in range(KC):
                            for i, (a, b) in enumerate(PASSES):
                                last = nc.tensor.matmul(ps[:, 2 * h + c], wkv[:, 0, a, k, P * h:P * (h + 1)],
                                                        ctx_parts[:, b, k, 512 * c:512 * (c + 1)],
                                                        start=(k == 0 and i == 0), stop=(k == KC - 1 and i == 2))
                        last.then_inc(k_product, 1)
                for b in range(B):
                    if b >= 4:
                        pe.wait_ge(v_stored, 2 * (b - 3))
                    for e in range(2):
                        for k in range(KC):
                            w = [wkv[:, 1, i, k, :].rearrange("c (p e d) -> c e p d", e=2, d=HD)[:, e] for i in range(2)]
                            for i, (a, m) in enumerate(PASSES):
                                last = nc.tensor.matmul(ps[KEYS * e:KEYS * (e + 1), 4 + b % 4, 0:PAIRS * HD],
                                                        ctx_parts[:, a, k, KEYS * b:KEYS * (b + 1)], w[m],
                                                        start=(k == 0 and i == 0), stop=(k == KC - 1 and i == 2))
                    last.then_inc(v_product, 1)

            @block.vector
            def _(dve):
                dve.wait_ge(split_hi, 1)
                nc.vector.tensor_tensor(ctx_parts[:, 1], ctx_t[:, :, :], ctx_parts[:, 0], ALU.subtract).then_inc(split_lo, 1)
                for n in range(NW):
                    dve.wait_ge(split_hi, n + 2)
                    nc.vector.scalar_tensor_tensor(targets[n][:, 1], w_raw[:, n], WS, targets[n][:, 0],
                                                   ALU.mult, ALU.subtract).then_inc(split_lo, 1)
                if layer == 0:
                    dve.wait_ge(loaded["bias"], 16 * 5)
                    for n in range(2 * KC):
                        h, c = n // 2, n % 2
                        dve.wait_ge(k_hi, n + 1)
                        raw = w_raw[:, n, :, :].rearrange("p k n -> p (k n)")
                        nc.vector.tensor_scalar(raw, ps[:, n], 1.0 / WS, key_bias[:, h:h + 1], ALU.mult, ALU.add).then_inc(k_lo, 1)
                        dve.wait_ge(k_lo, 2 * n + 1)
                        nc.vector.tensor_tensor(k_parts[:, 1, h, 512 * c:512 * (c + 1)], raw,
                                                k_parts[:, 0, h, 512 * c:512 * (c + 1)], ALU.subtract).then_inc(k_lo, 1)
                    dve.wait_ge(k_lo, 4 * KC)
                else:
                    dve.wait_ge(split_lo, 1)
                for part in range(2):
                    for h in range(KC):
                        keys = bc(k_parts[:, part, h, :].rearrange("p (b k) -> p b k", b=B), 2, HPP)
                        nc.vector.tensor_tensor(kbd[:, part, :, h], keys, bc(g.head_mask[:, :, :], 1, B), ALU.mult)
                dve.wait_ge(ones_set, 2)
                if layer == 0:
                    for b in range(B):
                        dve.wait_ge(v_product, b + 1)
                        for e in range(2):
                            rows = slice(KEYS * e, KEYS * (e + 1))
                            nc.vector.scalar_tensor_tensor(
                                vbd[rows, b, :, VC * e:VC * e + HD],
                                ps[rows, 4 + b % 4, 0:PAIRS * HD].rearrange("p (a d) -> p a d", d=HD), 1.0 / WS,
                                v_bias[rows], ALU.mult, ALU.add).then_inc(v_stored, 1)
                    for b in range(B):
                        dve.wait_ge(x_loaded[b], 16)
                        for t in range(TPB):
                            last = nc.vector.bn_stats(g.stats[:, TPB * b + t, :], g.res[:, TPB * b + t, :])
                    last.then_inc(stats_done, 1)
                    dve.wait_ge(stats_done, 1)
                else:
                    dve.wait_ge(loaded["ctx_dup"], 32)
                    for e in range(2):
                        rows = slice(KEYS * e, KEYS * (e + 1))
                        nc.vector.tensor_copy(vbd[rows, :, :, VC * e:VC * e + HD],
                                              ctx_dup[rows].rearrange("p b (a e d) -> p b e a d", e=2, d=HD)[:, :, e])
                finish_stats(nc, dve, g, "dve", sems)


def attention(nc, g, io, layer, res, kbd, vbd, wq, wo):
    LN, HT, QP, SC, SM, PT, AV, OT, OUT = range(9)
    EX = SM
    pipe = Tiles(NT, 4, 12, OUT)
    with Stage(nc, f"attn{layer}") as st:
        normed = st.sb("normed", [P, 2, D], F32)
        h_parts = st.sb("h_parts", [P, 4, 2, KC, P], F16)
        probs = st.sb("probs", [P, 4, HEADS, KEYS], F32)
        probs_t = st.sb("probs_t", [P, 2, PAIRS, P], F32)
        row_max = st.sb("row_max", [P, 4, HEADS], F32)
        row_sum = st.sb("row_sum", [P, 2, HEADS], F32)
        heads_out = st.sb("heads_out", [P, 2, D], F32)
        o_parts = st.sb("o_parts", [P, 2, 2, KC, P], F16)
        if layer == 0:
            q_parts = st.sb("q_parts", [P, 2, 2, KC, P], F16)
            q_f32 = st.sb("q_f32", [P, KC, P], F32)
            fill = st.sb("fill", [P, HEADS, KEYS], F32)
            mask = st.sb("mask", [P, TPB, KEYS], F32)
        else:
            mask = st.sb("mask", [P, TPB, KEYS], I32)
            mask_fill = st.sb("mask_fill", [P, TPB, KEYS], BF16)
        mask_loaded = [st.sem(f"mask_loaded{t}") for t in range(TPB)]
        s = {k: st.sem(k) for k in (
            "fill_ready", "normed", "h_t", "h_hi", "h_lo", "q", "q_hi", "q_f32", "q_lo", "scores",
            "masked", "fill", "filled", "max", "shifted", "exp", "p_t", "p_t_out", "av", "recip", "heads", "o_t",
            "o_hi", "o_lo", "projected", "bias", "residual", "stored")}
        ps = g.psum
        ps_h = ps[:, 0, 0:D].rearrange("p (k n) -> p k n", k=KC)
        ps_q = ps[:, 7, 0:D].rearrange("p (k n) -> p k n", k=KC)
        ps_s = ps[:, 1:3, :].rearrange("p a (h k) -> p (a h) k", k=KEYS)
        ps_p = ps[:, 3:5, :].rearrange("p a (r q) -> p (a r) q", q=P)
        ps_v = ps[:, 5, 0:PAIRS * 2 * VC].rearrange("p (h c) -> p h c", c=VC)
        ps_o = ps[:, 6, 0:D].rearrange("p (k n) -> p k n", k=KC)
        ps_y = ps[:, 6, D:2 * D]
        with nc.Block() as block:
            @block.sync
            def _(sp):
                by_tile = io[f"mask{layer}"].rearrange("(t p) k -> t p k", p=P)
                for t in range(TPB):
                    sp.dma_start(mask[:, t], by_tile[t]).then_inc(mask_loaded[t], 16)
                with sp.Fori(1, B) as c:
                    for t in range(TPB):
                        sp.wait_ge(s["masked" if layer == 0 else "fill_ready"], (c - 1) * TPB + t + 1)
                        sp.dma_start(mask[:, t], by_tile[c * TPB + t]).then_inc(mask_loaded[t], 16)
                    if layer == 0:
                        sp.wait_ge(s["residual"], c * TPB)
                        sp.dma_start(io["x1_spill"][:, c - 1], res[:, bass.ds((c - 1) * TPB, TPB), :]).then_inc(s["stored"], 16)
                if layer == 0:
                    sp.wait_ge(s["residual"], B * TPB)
                    sp.dma_start(io["x1_spill"][:, B - 1], res[:, (B - 1) * TPB:, :]).then_inc(s["stored"], 16)
                    sp.wait_ge(s["stored"], 16 * B)

            @block.gpsimd
            def _(pool):
                def step(r, j, live):
                    n = TPB * r + j
                    if live(HT):
                        u = n - HT
                        pool.wait_ge(s["normed"], u + 1)
                        nc.gpsimd.tensor_tensor(res[:, u, :], res[:, u, :], g.out_bias[:, :], ALU.add).then_inc(s["bias"], 1)
                    if layer == 0 and live(SM):
                        u, slot = n - SM, (j - SM) % 4
                        pool.wait_ge(s["max"], u + 1)
                        nc.gpsimd.tensor_tensor(probs[:, slot], probs[:, slot], bc(row_max[:, slot], 2, KEYS),
                                                ALU.subtract).then_inc(s["shifted"], 1)
                pipe.run(pool, step)

            @block.tensor
            def _(pe):
                def step(r, j, live):
                    n = TPB * r + j
                    if live(HT):
                        u = n - HT
                        pe.wait_ge(s["normed"], u + 1)
                        wait(pe, s["h_lo"], u)
                        for k in range(KC):
                            last = nc.tensor.transpose(ps_h[:, k], normed[:, (j - HT) % 2, P * k:P * (k + 1)], g.ident32[:, :])
                        last.then_inc(s["h_t"], 1)
                    if layer == 0 and live(QP):
                        u = n - QP
                        pe.wait_ge(s["h_lo"], u + 1)
                        wait(pe, s["q_f32"], u)
                        for m in range(KC):
                            for k in range(KC):
                                for i, (a, b) in enumerate(PASSES):
                                    last = nc.tensor.matmul(ps_q[:, m], wq[:, a, k, P * m:P * (m + 1)],
                                                            h_parts[:, (j - QP) % 4, b, k], start=(k == 0 and i == 0),
                                                            stop=(k == KC - 1 and i == 2))
                        last.then_inc(s["q"], 1)
                    if live(OUT):
                        u = n - OUT
                        pe.wait_ge(s["o_lo"], u + 1)
                        for k in range(KC):
                            for i, (a, b) in enumerate(PASSES):
                                last = nc.tensor.matmul(ps_y, o_parts[:, (j - OUT) % 2, a, k], wo[:, b, k],
                                                        start=(k == 0 and i == 0), stop=(k == KC - 1 and i == 2))
                        last.then_inc(s["projected"], 1)
                    if live(SC):
                        u = n - SC
                        batch = r + (j - SC) // TPB
                        pe.wait_ge(s["q_lo" if layer == 0 else "h_lo"], u + 1)
                        wait(pe, s["masked" if layer == 0 else "shifted"], u)
                        q = q_parts[:, (j - SC) % 2] if layer == 0 else h_parts[:, (j - SC) % 4]
                        for m in range(KC):
                            out = ps[:, 1 + m, :]
                            if layer == 1:
                                pe.wait_ge(s["fill_ready"], u + 1)
                                nc.tensor.matmul(out, g.identb[:, :], bc(mask_fill[:, (j - SC) % 4], 1, HPP), start=True, stop=False)
                            for i, (a, b) in enumerate(PASSES):
                                last = nc.tensor.matmul(out, q[:, a, m], kbd[:, b, batch, m],
                                                        start=(layer == 0 and i == 0), stop=(i == 2))
                        last.then_inc(s["scores"], 1)
                    if live(PT):
                        u, slot = n - PT, (j - PT) % 4
                        pe.wait_ge(s["exp"], u + 1)
                        wait(pe, s["p_t_out"], u)
                        for a in range(PAIRS):
                            pair = probs[:, slot, 2 * a:2 * a + 2, :].rearrange("p h k -> p (h k)")
                            last = nc.tensor.transpose(ps_p[:, a], pair, g.ident32[:, :])
                        last.then_inc(s["p_t"], 1)
                    if live(AV):
                        u = n - AV
                        batch = r + (j - AV) // TPB
                        pe.wait_ge(s["p_t_out"], u + 1)
                        wait(pe, s["heads"], u)
                        for a in range(PAIRS):
                            last = nc.tensor.matmul(ps_v[:, 2 * a:2 * a + 2, :].rearrange("p h c -> p (h c)"),
                                                    probs_t[:, (j - AV) % 2, a], vbd[:, batch, a], start=True, stop=True)
                        last.then_inc(s["av"], 1)
                    if live(OT):
                        u = n - OT
                        pe.wait_ge(s["heads"], u + 1)
                        wait(pe, s["residual"], u)
                        for k in range(KC):
                            last = nc.tensor.transpose(ps_o[:, k], heads_out[:, (j - OT) % 2, P * k:P * (k + 1)], g.ident32[:, :])
                        last.then_inc(s["o_t"], 1)
                pipe.run(pe, step)

            @block.scalar
            def _(act):
                def step(r, j, live):
                    n = TPB * r + j
                    if live(HT):
                        u = n - HT
                        act.wait_ge(s["h_t"], u + 1)
                        wait(act, s["q" if layer == 0 else "scores"], u - 3)
                        nc.scalar.copy(h_parts[:, (j - HT) % 4, 0], ps_h[:, :, :]).then_inc(s["h_hi"], 1)
                    if layer == 0 and live(QP):
                        u = n - QP
                        act.wait_ge(s["q_f32"], u + 1)
                        wait(act, s["scores"], u - 1)
                        nc.scalar.copy(q_parts[:, (j - QP) % 2, 0], q_f32[:, :, :]).then_inc(s["q_hi"], 1)
                    if live(EX):
                        u, slot = n - EX, (j - EX) % 4
                        act.wait_ge(s["shifted"], u + 1)
                        nc.scalar.activation(probs[:, slot], probs[:, slot], ACT.Exp,
                                             scale=0.25 if layer == 0 else 1.0 / 16.0).then_inc(s["exp"], 1)
                    if live(PT):
                        u = n - PT
                        act.wait_ge(s["p_t"], u + 1)
                        wait(act, s["av"], u - 1)
                        nc.scalar.copy(probs_t[:, (j - PT) % 2], ps_p[:, :, :]).then_inc(s["p_t_out"], 1)
                    if live(OT):
                        u = n - OT
                        act.wait_ge(s["o_t"], u + 1)
                        wait(act, s["projected"], u - 1)
                        nc.scalar.copy(o_parts[:, (j - OT) % 2, 0], ps_o[:, :, :]).then_inc(s["o_hi"], 1)
                pipe.run(act, step)

            @block.vector
            def _(dve):
                def step(r, j, live):
                    n = TPB * r + j
                    if live(LN):
                        u = n
                        wait(dve, s["h_t"], u - 1)
                        nc.vector.tensor_scalar(normed[:, j % 2], res[:, u, :], g.mean[:, bass.ds(u, 1)], g.rstd[:, bass.ds(u, 1)],
                                                ALU.subtract, ALU.mult).then_inc(s["normed"], 1)
                    if layer == 1 and live(LN):
                        u, slot = n, j % 4
                        dve.wait_ge(mask_loaded[slot], 16 * r + 16)
                        wait(dve, s["scores"], u - 3)
                        nc.vector.tensor_scalar(mask_fill[:, slot], mask[:, slot], 0.0, -1e20, ALU.is_equal,
                                                ALU.mult).then_inc(s["fill_ready"], 1)
                    if live(HT):
                        u, slot = n - HT, (j - HT) % 4
                        dve.wait_ge(s["h_hi"], u + 1)
                        nc.vector.tensor_tensor(h_parts[:, slot, 1], ps_h[:, :, :], h_parts[:, slot, 0], ALU.subtract).then_inc(s["h_lo"], 1)
                    if layer == 0 and live(QP):
                        u = n - QP
                        dve.wait_ge(s["q"], u + 1)
                        wait(dve, s["q_lo"], u)
                        for m in range(KC):
                            last = nc.vector.tensor_scalar(q_f32[:, m], ps_q[:, m], 1.0 / WS, g.q_bias[:, m:m + 1],
                                                           ALU.mult, ALU.add)
                        last.then_inc(s["q_f32"], 1)
                    if live(OUT):
                        u = n - OUT
                        dve.wait_ge(s["projected"], u + 1)
                        dve.wait_ge(s["bias"], u + 1)
                        nc.vector.scalar_tensor_tensor(res[:, u, :], ps_y, 1.0 / WS, res[:, u, :], ALU.mult,
                                                       ALU.add).then_inc(s["residual"], 1)
                        dve.wait_ge(s["residual"], u + 1)
                        nc.vector.bn_stats(g.stats[:, u, :], res[:, u, :])
                    if live(SC):
                        u, slot = n - SC, (j - SC) % 4
                        dve.wait_ge(s["scores"], u + 1)
                        wait(dve, s["p_t"], u - 3)
                        if layer == 0:
                            batch = r + (j - SC) // TPB
                            dve.wait_ge(mask_loaded[slot], 16 * batch + 16)
                            t = probs[:, slot]
                            nc.vector.tensor_tensor(t, ps_s[:, :, :], bc(mask[:, slot], 1, HEADS), ALU.mult).then_inc(s["masked"], 1)
                            dve.wait_ge(s["masked"], u + 1)
                            wait(dve, s["filled"], u)
                            nc.vector.tensor_scalar(fill[:, :, :], t, 0.0, -4e9, ALU.is_equal, ALU.mult).then_inc(s["fill"], 1)
                            dve.wait_ge(s["fill"], u + 1)
                            nc.vector.tensor_tensor(t, t, fill[:, :, :], ALU.add).then_inc(s["filled"], 1)
                            dve.wait_ge(s["filled"], u + 1)
                            nc.vector.tensor_reduce(row_max[:, slot], t, AX.X, ALU.max).then_inc(s["max"], 1)
                        else:
                            nc.vector.tensor_reduce(row_max[:, slot], ps_s[:, :, :], AX.X, ALU.max).then_inc(s["max"], 1)
                            dve.wait_ge(s["max"], u + 1)
                            nc.vector.tensor_tensor(probs[:, slot], ps_s[:, :, :], bc(row_max[:, slot], 2, KEYS),
                                                    ALU.subtract).then_inc(s["shifted"], 1)
                    if layer == 0 and live(QP):
                        u = n - QP
                        dve.wait_ge(s["q_hi"], u + 1)
                        nc.vector.tensor_tensor(q_parts[:, (j - QP) % 2, 1], q_f32[:, :, :], q_parts[:, (j - QP) % 2, 0],
                                                ALU.subtract).then_inc(s["q_lo"], 1)
                    if live(AV):
                        u, slot = n - AV, (j - AV) % 2
                        dve.wait_ge(s["av"], u + 1)
                        nc.vector.reciprocal(row_sum[:, slot], ps_v[:, :, HD]).then_inc(s["recip"], 1)
                        dve.wait_ge(s["recip"], u + 1)
                        wait(dve, s["o_t"], u - 1)
                        nc.vector.tensor_tensor(heads_out[:, slot].rearrange("p (h d) -> p h d", d=HD), ps_v[:, :, 0:HD],
                                                bc(row_sum[:, slot], 2, HD), ALU.mult).then_inc(s["heads"], 1)
                    if live(OT):
                        u, slot = n - OT, (j - OT) % 2
                        dve.wait_ge(s["o_hi"], u + 1)
                        nc.vector.tensor_tensor(o_parts[:, slot, 1], ps_o[:, :, :], o_parts[:, slot, 0], ALU.subtract).then_inc(s["o_lo"], 1)
                pipe.run(dve, step)


NC = B
PAIR_I = NI // 2
(M_H, M_G, M_U, M_V, M_O, S_H, INV_H, K_G, S_G, K_U, K_V, K_O, K_OUT, TMP, S_U, S_V) = range(16)


def col(g, c):
    return g.scal[:, c:c + 1]


def scale_of(chain, nc, g, peak, unit, out):
    if unit is not None:
        chain(nc.vector.tensor_scalar(col(g, TMP), col(g, peak), col(g, unit), 1.0 / QMAX, ALU.mult, ALU.mult))
    else:
        chain(nc.vector.tensor_scalar(col(g, TMP), col(g, peak), 1.0 / QMAX, None, ALU.mult))
    chain(nc.vector.tensor_scalar(col(g, out), col(g, TMP), 1e-12, None, ALU.max))


def ffn_prep(nc, g, io, w_gu, w_d, h_parts_t, scratch):
    NB = NI * D // QB
    WCOLS = NI * D
    with Stage(nc, "quant") as st:
        raw = scratch[:, 0:6 * WCOLS].bitcast(F32).rearrange("p (t n) -> p t n", t=3)
        ratio = scratch[:, 6 * WCOLS:8 * WCOLS].bitcast(F32)
        w_parts = scratch[:, 8 * WCOLS:10 * WCOLS].bitcast(F16).rearrange("p (a n) -> p a n", a=2)
        block_max = st.sb("block_max", [P, NB], F32)
        block_step = st.sb("block_step", [P, NB], F32)
        block_inv = st.sb("block_inv", [P, NB], F32)
        w_int = st.sb("w_int", [P, WCOLS], I16)
        shift = st.sb("shift", [P, NT], F32)
        peaks = st.sb("peaks", [P, NC], F32)
        row_peak = st.sb("row_peak", [P, 1], F32)
        h_int = st.sb("h_int", [P, 2, TPB, D], I16)
        h_split = st.sb("h_split", [P, 2, 2, TPB, D], F16)
        sems = (st.sem("stat_steps"), st.sem("var_ready"), st.sem("std_ready"), st.sem("rstd_ready"))
        s = {k: st.sem(k) for k in ("raw_loaded", "steps", "w_split", "w_t", "w_stored", "shift", "applied",
                                    "peak", "row_peak", "all_peak", "h_int", "h_hi", "h_lo", "h_t", "h_stored")}
        pipe = Tiles(NC, 2, 2, 1)
        ps16 = [g.psum[:, b, :].bitcast(F16) for b in range(8)]
        with nc.Block() as block:
            @block.sync
            def _(sp):
                for n, name in enumerate(("w_gate", "w_up")):
                    sp.dma_start(raw[:, n].rearrange("p (i d) -> p i d", d=D),
                                 io[f"L0_ffn_{name}"].rearrange("(i p) d -> p i d", p=P)).then_inc(s["raw_loaded"], 16)
                sp.dma_start(raw[:, 2].rearrange("p (r i) -> p r i", r=KC),
                             io["L0_ffn_w_down"].rearrange("(r p) i -> p r i", p=P)).then_inc(s["raw_loaded"], 16)
                sp.wait_ge(s["raw_loaded"], 48)

            @block.gpsimd
            def _(pool):
                pool.wait_ge(s["row_peak"], 1)
                nc.gpsimd.partition_all_reduce(col(g, M_H), row_peak[:, :], P, RMAX).then_inc(s["all_peak"], 1)

            @block.scalar
            def _(act):
                finish_stats(nc, act, g, "act", sems)
                act.wait_ge(s["shift"], 1)
                with act.Fori(0, NC) as c:
                    for t in range(TPB):
                        u = c * TPB + t
                        last = nc.scalar.activation(g.res[:, u, :], g.res[:, u, :], ACT.Identity,
                                                    bias=shift[:, bass.ds(u, 1)], scale=g.rstd[:, bass.ds(u, 1)])
                    last.then_inc(s["applied"], 1)
                for n in range(12):
                    act.wait_ge(s["w_t"], n + 1)
                    src = ps16[4 + n % 4][:, 0:FF]
                    part, q = (n % 4) // 2, n % 2
                    if n < 8:
                        dst = w_gu[:, part, n // 4, q, :]
                    else:
                        dst = w_d[:, part, 3 * q:3 * q + 3, :].rearrange("p i d -> p (i d)")
                    nc.scalar.copy(dst, src).then_inc(s["w_stored"], 1)

                def step(r, j, live):
                    if live(0):
                        c = 2 * r + j
                        act.wait_ge(s["h_int"], c + 1)
                        wait(act, s["h_t"], c - 1)
                        nc.scalar.copy(h_split[:, j, 0], h_int[:, j]).then_inc(s["h_hi"], 1)
                    if live(1):
                        c, slot = 2 * r + j - 1, (j - 1) % 2
                        act.wait_ge(s["h_t"], c + 1)
                        for part in range(2):
                            last = nc.scalar.copy(h_parts_t[:, part, :, bass.ds(c * S, S)],
                                                  ps16[2 * slot + part].rearrange("p (k n) -> p k n", k=KC))
                        last.then_inc(s["h_stored"], 1)
                pipe.run(act, step)

            @block.tensor
            def _(pe):
                for t in range(3):
                    pe.wait_ge(s["w_split"], t + 1)
                    for n in range(4):
                        part, q = n // 2, n % 2
                        wait(pe, s["w_stored"], 4 * (t - 1) + n + 1)
                        for m in range(6):
                            if t < 2:
                                src = w_parts[:, part, D * m + P * q:D * m + P * (q + 1)]
                            else:
                                at = FF * (m % 2) + P * (3 * q + m // 2)
                                src = w_parts[:, part, at:at + P]
                            last = nc.tensor.transpose(ps16[4 + n][:, P * m:P * (m + 1)], src, g.ident16[:, :])
                        last.then_inc(s["w_t"], 1)

                def step(r, j, live):
                    if live(1):
                        c, slot = 2 * r + j - 1, (j - 1) % 2
                        pe.wait_ge(s["h_lo"], c + 1)
                        wait(pe, s["h_stored"], c - 1)
                        for part in range(2):
                            for k in range(KC):
                                for t in range(TPB):
                                    at = k * S + t * P
                                    last = nc.tensor.transpose(ps16[2 * slot + part][:, at:at + P],
                                                               h_split[:, slot, part, t, P * k:P * (k + 1)], g.ident16[:, :])
                        last.then_inc(s["h_t"], 1)
                pipe.run(pe, step)

            @block.vector
            def _(dve):
                finish_stats(nc, dve, g, "dve", sems)
                dve.wait_ge(sems[3], 1)
                chain = Chain(dve, s["steps"])
                chain(nc.vector.scalar_tensor_tensor(shift[:, :], g.mean[:, :], -1.0, g.rstd[:, :], ALU.mult, ALU.mult))
                dve.sem_inc(s["shift"], 1)
                dve.wait_ge(s["raw_loaded"], 48)
                for t in range(3):
                    blocks = raw[:, t].rearrange("p (b q) -> p b q", q=QB)
                    chain(nc.vector.tensor_reduce(block_max[:, :], blocks, AX.X, ALU.max, apply_absolute_value=True))
                    chain(nc.vector.tensor_scalar(block_step[:, :], block_max[:, :], 1.0 / 7.0, 1e-12, ALU.mult, ALU.max))
                    chain(nc.vector.reciprocal(block_inv[:, :], block_step[:, :]))
                    r3 = ratio.rearrange("p (b q) -> p b q", q=QB)
                    i3 = w_int[:, :].rearrange("p (b q) -> p b q", q=QB)
                    chain(nc.vector.tensor_tensor(i3, blocks, bc(block_inv[:, :], 2, QB), ALU.mult))
                    chain(nc.vector.tensor_tensor(r3, i3, bc(block_step[:, :], 2, QB), ALU.mult))
                    if t:
                        dve.wait_ge(s["w_t"], 4 * t)
                    chain(nc.vector.tensor_scalar(w_parts[:, 0], ratio, WS, None, ALU.mult))
                    nc.vector.scalar_tensor_tensor(w_parts[:, 1], ratio, WS, w_parts[:, 0], ALU.mult,
                                                   ALU.subtract).then_inc(s["w_split"], 1)
                    dve.wait_ge(s["w_split"], t + 1)
                with dve.Fori(0, NC) as c:
                    dve.wait_ge(s["applied"], c + 1)
                    nc.vector.tensor_reduce(peaks[:, bass.ds(c, 1)], g.res[:, bass.ds(c * TPB, TPB), :], AX.XY, ALU.max,
                                            apply_absolute_value=True).then_inc(s["peak"], 1)
                dve.wait_ge(s["peak"], NC)
                nc.vector.tensor_reduce(row_peak[:, :], peaks[:, :], AX.X, ALU.max).then_inc(s["row_peak"], 1)
                dve.wait_ge(s["all_peak"], 1)
                scale_of(chain, nc, g, M_H, None, S_H)
                chain(nc.vector.reciprocal(col(g, INV_H), col(g, S_H)))

                def step(r, j, live):
                    if live(0):
                        c = 2 * r + j
                        wait(dve, s["h_lo"], c - 1)
                        nc.vector.tensor_scalar(h_int[:, j], g.res[:, bass.ds(c * TPB, TPB), :], col(g, INV_H), None,
                                                ALU.mult).then_inc(s["h_int"], 1)
                        dve.wait_ge(s["h_hi"], c + 1)
                        nc.vector.tensor_tensor(h_split[:, j, 1], h_int[:, j], h_split[:, j, 0], ALU.subtract).then_inc(s["h_lo"], 1)
                pipe.run(dve, step)


def project_in(nc, pe, g, w_gu, which, i, bank, h_parts_t, c):
    for k in range(KC):
        for m, (a, b) in enumerate(PASSES):
            last = nc.tensor.matmul(g.psum[:, bank, :], w_gu[:, a, which, k, P * i:P * (i + 1)],
                                    h_parts_t[:, b, k, bass.ds(c * S, S)],
                                    start=(k == 0 and m == 0), stop=(k == KC - 1 and m == 2))
    return last


def ffn_peaks(nc, g, w_gu, h_parts_t):
    pipe = Tiles(NC, 1, 1, 0)
    SLOTS = 3
    with Stage(nc, "peaks") as st:
        peaks = st.sb("peaks", [P, 2, NC * PAIR_I], F32)
        row_peak = st.sb("row_peak", [P, 2], F32)
        s = {k: st.sem(k) for k in ("product", "peak", "row_peak", "all_peak", "steps")}
        with nc.Block() as block:
            @block.tensor
            def _(pe):
                def step(r, j, live):
                    for n in range(2 * PAIR_I):
                        wait(pe, s["peak"], 2 * PAIR_I * r + n - SLOTS + 1)
                        for e in range(2):
                            last = project_in(nc, pe, g, w_gu, n // PAIR_I, 2 * (n % PAIR_I) + e, 2 * (n % SLOTS) + e, h_parts_t, r)
                        last.then_inc(s["product"], 1)
                pipe.run(pe, step)

            @block.gpsimd
            def _(pool):
                pool.wait_ge(s["row_peak"], 1)
                nc.gpsimd.partition_all_reduce(g.scal[:, M_G:M_U + 1], row_peak[:, :], P, RMAX).then_inc(s["all_peak"], 1)

            @block.vector
            def _(dve):
                def step(r, j, live):
                    for n in range(2 * PAIR_I):
                        dve.wait_ge(s["product"], 2 * PAIR_I * r + n + 1)
                        slot = 2 * (n % SLOTS)
                        nc.vector.tensor_reduce(peaks[:, n // PAIR_I, bass.ds(r * PAIR_I + n % PAIR_I, 1)], g.psum[:, slot:slot + 2, :],
                                                AX.XY, ALU.max, apply_absolute_value=True).then_inc(s["peak"], 1)
                pipe.run(dve, step)
                dve.wait_ge(s["peak"], 2 * PAIR_I * NC)
                nc.vector.tensor_reduce(row_peak[:, :], peaks[:, :, :], AX.X, ALU.max).then_inc(s["row_peak"], 1)
                dve.wait_ge(s["all_peak"], 1)
                chain = Chain(dve, s["steps"])
                chain(nc.vector.tensor_scalar(col(g, S_H), col(g, S_H), 1.0 / WS, None, ALU.mult))
                for peak, step_, k in ((M_G, S_G, K_G), (M_U, S_U, K_U)):
                    scale_of(chain, nc, g, peak, S_H, step_)
                    chain(nc.vector.reciprocal(col(g, k), col(g, step_)))
                    chain(nc.vector.tensor_scalar(col(g, k), col(g, k), col(g, S_H), None, ALU.mult))


def ffn_gate(nc, g, w_gu, h_parts_t, gate_int):
    pipe = Tiles(NC, 1, 1, 0)
    with Stage(nc, "gate") as st:
        sig = st.sb("sig", [P, PAIR_I, 2, S], F32)
        sig_int = st.sb("sig_int", [P, PAIR_I, 2, S], U16)
        peaks = st.sb("peaks", [P, NC * PAIR_I], F32)
        row_peak = st.sb("row_peak", [P, 1], F32)
        s = {k: st.sem(k) for k in ("product", "gate_int", "held", "sig", "sig_int", "value", "peak", "row_peak", "all_peak", "steps")}
        with nc.Block() as block:
            @block.tensor
            def _(pe):
                def step(r, j, live):
                    for n in range(PAIR_I):
                        wait(pe, s["gate_int"], PAIR_I * (r - 1) + n + 1)
                        for e in range(2):
                            last = project_in(nc, pe, g, w_gu, 0, 2 * n + e, 2 * n + e, h_parts_t, r)
                        last.then_inc(s["product"], 1)
                pipe.run(pe, step)

            @block.scalar
            def _(act):
                def step(r, j, live):
                    for n in range(PAIR_I):
                        u = PAIR_I * r + n
                        act.wait_ge(s["product"], u + 1)
                        kept = gate_int(n)[:, :, bass.ds(r * S, S)]
                        nc.scalar.activation(kept, g.psum[:, 2 * n:2 * n + 2, :], ACT.Identity, scale=col(g, K_G)).then_inc(s["gate_int"], 1)
                        act.wait_ge(s["gate_int"], u + 1)
                        wait(act, s["peak"], u - PAIR_I + 1)
                        act.sem_inc(s["held"], 1)
                        nc.scalar.activation(sig[:, n], kept, ACT.Sigmoid, scale=col(g, S_G)).then_inc(s["sig"], 1)
                pipe.run(act, step)

            @block.gpsimd
            def _(pool):
                pool.wait_ge(s["row_peak"], 1)
                nc.gpsimd.partition_all_reduce(col(g, M_V), row_peak[:, :], P, RMAX).then_inc(s["all_peak"], 1)

            @block.vector
            def _(dve):
                def peak_of(r, n):
                    dve.wait_ge(s["sig_int"], PAIR_I * r + n + 1)
                    nc.vector.tensor_tensor(sig[:, n], gate_int(n)[:, :, bass.ds(r * S, S)], sig_int[:, n],
                                            ALU.mult).then_inc(s["value"], 1)
                    dve.wait_ge(s["value"], PAIR_I * r + n + 1)
                    nc.vector.tensor_reduce(peaks[:, bass.ds(r * PAIR_I + n, 1)], sig[:, n], AX.XY, ALU.max,
                                            apply_absolute_value=True).then_inc(s["peak"], 1)

                def step(r, j, live):
                    for n in range(PAIR_I):
                        u = PAIR_I * r + n
                        dve.wait_ge(s["sig"], u + 1)
                        wait(dve, s["value"], u - PAIR_I + 1)
                        nc.vector.tensor_scalar(sig_int[:, n], sig[:, n], 65536.0, 65535.0, ALU.mult, ALU.min).then_inc(s["sig_int"], 1)
                        peak_of(r, n)
                pipe.run(dve, step)
                dve.wait_ge(s["peak"], PAIR_I * NC)
                nc.vector.tensor_reduce(row_peak[:, :], peaks[:, :], AX.X, ALU.max).then_inc(s["row_peak"], 1)
                dve.wait_ge(s["all_peak"], 1)
                chain = Chain(dve, s["steps"])
                chain(nc.vector.tensor_scalar(col(g, S_G), col(g, S_G), 1.0 / 65536.0, None, ALU.mult))
                scale_of(chain, nc, g, M_V, S_G, S_V)
                chain(nc.vector.reciprocal(col(g, K_V), col(g, S_V)))
                chain(nc.vector.tensor_scalar(col(g, K_V), col(g, K_V), col(g, S_G), None, ALU.mult))
                chain(nc.vector.tensor_scalar(col(g, S_G), col(g, S_G), 65536.0, None, ALU.mult))


def ffn_up(nc, g, io, w_gu, h_parts_t, gate_int):
    pipe = Tiles(NC, 1, 1, 0)
    with Stage(nc, "up") as st:
        up_int = st.sb("up_int", [P, PAIR_I, 2, S], I16)
        sig = st.sb("sig", [P, PAIR_I, 2, S], F32)
        sig_int = st.sb("sig_int", [P, 2, S], U16)
        peaks = st.sb("peaks", [P, NC * PAIR_I], F32)
        row_peak = st.sb("row_peak", [P, 1], F32)
        stored = [st.sem(f"up_stored{n}") for n in range(PAIR_I)]
        s = {k: st.sem(k) for k in ("product", "up_int", "sig", "sig_int", "gate_int", "value", "peak", "row_peak",
                                    "all_peak", "steps")}
        with nc.Block() as block:
            @block.sync
            def _(sp):
                with sp.Fori(0, NC) as c:
                    for n in range(PAIR_I):
                        sp.wait_ge(s["up_int"], c * PAIR_I + n + 1)
                        sp.dma_start(io["up_spill"][:, c, n], up_int[:, n]).then_inc(stored[n], 16)
                for n in range(PAIR_I):
                    sp.wait_ge(stored[n], 16 * NC)

            @block.tensor
            def _(pe):
                def step(r, j, live):
                    for n in range(PAIR_I):
                        wait(pe, s["up_int"], PAIR_I * (r - 1) + n + 1)
                        for e in range(2):
                            last = project_in(nc, pe, g, w_gu, 1, 2 * n + e, 2 * n + e, h_parts_t, r)
                        last.then_inc(s["product"], 1)
                pipe.run(pe, step)

            @block.scalar
            def _(act):
                def step(r, j, live):
                    for n in range(PAIR_I):
                        u = PAIR_I * r + n
                        wait(act, s["peak"], u - PAIR_I + 1)
                        nc.scalar.activation(sig[:, n], gate_int(n)[:, :, bass.ds(r * S, S)], ACT.Sigmoid,
                                             scale=col(g, S_G)).then_inc(s["sig"], 1)
                        act.wait_ge(s["product"], u + 1)
                        wait(act, s["value"], u - PAIR_I + 1)
                        wait(act, stored[n], 16 * r)
                        nc.scalar.activation(up_int[:, n], g.psum[:, 2 * n:2 * n + 2, :], ACT.Identity,
                                             scale=col(g, K_U)).then_inc(s["up_int"], 1)
                pipe.run(act, step)

            @block.gpsimd
            def _(pool):
                pool.wait_ge(s["row_peak"], 1)
                nc.gpsimd.partition_all_reduce(col(g, M_O), row_peak[:, :], P, RMAX).then_inc(s["all_peak"], 1)

            @block.vector
            def _(dve):
                def step(r, j, live):
                    for n in range(PAIR_I):
                        u = PAIR_I * r + n
                        kept = gate_int(n)[:, :, bass.ds(r * S, S)]
                        dve.wait_ge(s["sig"], u + 1)
                        wait(dve, s["gate_int"], u)
                        nc.vector.tensor_scalar(sig_int[:, :, :], sig[:, n], 65536.0, 65535.0, ALU.mult, ALU.min).then_inc(s["sig_int"], 1)
                        dve.wait_ge(s["sig_int"], u + 1)
                        nc.vector.scalar_tensor_tensor(kept, kept, col(g, K_V), sig_int[:, :, :], ALU.mult, ALU.mult).then_inc(s["gate_int"], 1)
                        dve.wait_ge(s["gate_int"], u + 1)
                        dve.wait_ge(s["up_int"], u + 1)
                        nc.vector.tensor_tensor(sig[:, n], kept, up_int[:, n], ALU.mult).then_inc(s["value"], 1)
                        dve.wait_ge(s["value"], u + 1)
                        nc.vector.tensor_reduce(peaks[:, bass.ds(r * PAIR_I + n, 1)], sig[:, n], AX.XY, ALU.max,
                                                apply_absolute_value=True).then_inc(s["peak"], 1)
                pipe.run(dve, step)
                dve.wait_ge(s["peak"], PAIR_I * NC)
                nc.vector.tensor_reduce(row_peak[:, :], peaks[:, :], AX.X, ALU.max).then_inc(s["row_peak"], 1)
                dve.wait_ge(s["all_peak"], 1)
                chain = Chain(dve, s["steps"])
                chain(nc.vector.tensor_scalar(col(g, S_V), col(g, S_V), col(g, S_U), None, ALU.mult))
                scale_of(chain, nc, g, M_O, S_V, K_OUT)
                chain(nc.vector.reciprocal(col(g, K_O), col(g, K_OUT)))
                chain(nc.vector.tensor_scalar(col(g, K_O), col(g, K_O), col(g, S_V), None, ALU.mult))
                chain(nc.vector.tensor_scalar(col(g, K_OUT), col(g, K_OUT), 1.0 / WS, None, ALU.mult))


def ffn_down(nc, g, io, w_d, gate_int, res):
    pipe = Tiles(NC, 2, 2, 0)
    with Stage(nc, "down") as st:
        up_int = st.sb("up_int", [P, PAIR_I, 2, S], I16)
        o_int = st.sb("o_int", [P, PAIR_I, 2, S], I16)
        o_parts = st.sb("o_parts", [P, PAIR_I, 2, 2, S], F16)
        x1 = st.sb("x1", [P, 2, TPB, D], F32)
        up_loaded = [st.sem(f"up_loaded{n}") for n in range(PAIR_I)]
        x1_loaded = [st.sem(f"x1_loaded{n}") for n in range(2)]
        s = {k: st.sem(k) for k in ("o_int", "o_hi", "o_lo", "used", "sum", "residual")}
        with nc.Block() as block:
            @block.sync
            def _(sp):
                def step(r, j, live):
                    c = 2 * r + j
                    wait(sp, s["residual"], c - 1)
                    sp.dma_start(x1[:, j], io["x1_spill"][:, c]).then_inc(x1_loaded[j], 16)
                    for n in range(PAIR_I):
                        wait(sp, s["o_int"], PAIR_I * (c - 1) + n + 1)
                        sp.dma_start(up_int[:, n], io["up_spill"][:, c, n]).then_inc(up_loaded[n], 16)
                pipe.run(sp, step)

            @block.tensor
            def _(pe):
                def step(r, j, live):
                    c = 2 * r + j
                    wait(pe, s["residual"], c - 1)
                    for n in range(PAIR_I):
                        pe.wait_ge(s["o_lo"], PAIR_I * c + n + 1)
                        for e in range(2):
                            for t in range(TPB):
                                for m, (a, b) in enumerate(PASSES):
                                    last = nc.tensor.matmul(g.psum[:, TPB * j + t, 0:D], o_parts[:, n, a, e, P * t:P * (t + 1)],
                                                            w_d[:, b, 2 * n + e, :], start=(n == 0 and e == 0 and m == 0),
                                                            stop=(n == PAIR_I - 1 and e == 1 and m == 2))
                        last.then_inc(s["used"], 1)
                pipe.run(pe, step)

            @block.scalar
            def _(act):
                def step(r, j, live):
                    c = 2 * r + j
                    for n in range(PAIR_I):
                        u = PAIR_I * c + n
                        act.wait_ge(s["o_int"], u + 1)
                        wait(act, s["used"], u - PAIR_I + 1)
                        nc.scalar.copy(o_parts[:, n, 0], o_int[:, n]).then_inc(s["o_hi"], 1)
                pipe.run(act, step)

            @block.vector
            def _(dve):
                def lows(u, n):
                    dve.wait_ge(s["o_hi"], u + 1)
                    nc.vector.tensor_tensor(o_parts[:, n, 1], o_int[:, n], o_parts[:, n, 0], ALU.subtract).then_inc(s["o_lo"], 1)

                def step(r, j, live):
                    c = 2 * r + j
                    for n in range(PAIR_I):
                        u = PAIR_I * c + n
                        dve.wait_ge(up_loaded[n], 16 * c + 16)
                        wait(dve, s["o_lo"], u - PAIR_I + 1)
                        nc.vector.scalar_tensor_tensor(o_int[:, n], gate_int(n)[:, :, bass.ds(c * S, S)], col(g, K_O), up_int[:, n],
                                                       ALU.mult, ALU.mult).then_inc(s["o_int"], 1)
                        if n:
                            lows(u - 1, n - 1)
                    lows(PAIR_I * c + PAIR_I - 1, PAIR_I - 1)
                    if not (isinstance(c, int) and c == 0):
                        residual(r if j else r - 1, 1 - j)

                def residual(r, j):
                    c = 2 * r + j
                    dve.wait_ge(s["used"], PAIR_I * c + PAIR_I)
                    dve.wait_ge(x1_loaded[j], 16 * r + 16)
                    for t in range(TPB):
                        nc.vector.scalar_tensor_tensor(res[:, c * TPB + t, :], g.psum[:, TPB * j + t, 0:D], col(g, K_OUT), x1[:, j, t],
                                                       ALU.mult, ALU.add).then_inc(s["sum"], 1)
                    for t in range(TPB):
                        dve.wait_ge(s["sum"], TPB * c + t + 1)
                        last = nc.vector.bn_stats(g.stats[:, c * TPB + t, :], res[:, c * TPB + t, :])
                    last.then_inc(s["residual"], 1)
                pipe.run(dve, step)
                residual(NC // 2 - 1, 1)


def moe_prep(nc, g, io, res, h_t):
    HT, LO = range(1, 3)
    NX = NE * NT
    pipe = Tiles(NT, 4, 8, LO)
    with Stage(nc, "route") as st:
        normed = st.sb("normed", [P, 4, D], F32)
        gate_raw = st.sb("gate_raw", [P, KC, NE], F32)
        gate_parts = st.sb("gate_parts", [P, 2, KC, NE], F16)
        e_bias = st.sb("e_bias", [P, NE], F32)
        scores = st.sb("scores", [P, NT, NE], F32)
        choice = st.sb("choice", [P, NT, NE], F32)
        rank = st.sb("rank", [P, NT, NE], F32)
        wins = st.sb("wins", [P, NT, NE], F32)
        high = st.sb("high", [P, NT, GROUPS, 2], F32)
        low = st.sb("low", [P, NT, GROUPS, 2], F32)
        group_sum = st.sb("group_sum", [P, NT, GROUPS], F32)
        second = st.sb("second", [P, NT, GROUPS], F32)
        group_rank = st.sb("group_rank", [P, NT, GROUPS], F32)
        total = st.sb("total", [P, NT], F32)
        sems = (st.sem("stat_steps"), st.sem("var_ready"), st.sem("std_ready"), st.sem("rstd_ready"))
        s = {k: st.sem(k) for k in ("loaded", "gate_hi", "gate_lo", "normed", "h_t", "h_hi", "h_lo", "logits",
                                    "logits_out", "scores", "steps")}
        with nc.Block() as block:
            @block.sync
            def _(sp):
                sp.dma_start(gate_raw[:, :, :], io["moe_gate_T"].rearrange("(k p) e -> p k e", p=P)).then_inc(s["loaded"], 16)
                sp.dma_start(e_bias[:, :], io["moe_e_bias"].rearrange("(a n) -> a n", a=1).to_broadcast([P, NE])).then_inc(s["loaded"], 16)
                sp.wait_ge(s["loaded"], 32)

            @block.tensor
            def _(pe):
                def step(r, j, live):
                    n = 4 * r + j
                    if live(HT):
                        u, slot = n - HT, (j - HT) % 4
                        pe.wait_ge(s["normed"], u + 1)
                        wait(pe, s["h_lo"], u - 3)
                        for k in range(KC):
                            last = nc.tensor.transpose(g.psum[:, slot, P * k:P * (k + 1)], normed[:, slot, P * k:P * (k + 1)], g.ident32[:, :])
                        last.then_inc(s["h_t"], 1)
                    if live(LO):
                        u, slot = n - LO, (j - LO) % 4
                        pe.wait_ge(s["h_lo"], u + 1)
                        wait(pe, s["logits_out"], u - 3)
                        if isinstance(u, int) and u == 0:
                            pe.wait_ge(s["gate_lo"], 1)
                        for k in range(KC):
                            for i, (a, b) in enumerate(PASSES):
                                last = nc.tensor.matmul(g.psum[:, 4 + slot, 0:NE], h_t[:, a, k, bass.ds(u * P, P)], gate_parts[:, b, k],
                                                        start=(k == 0 and i == 0), stop=(k == KC - 1 and i == 2))
                        last.then_inc(s["logits"], 1)
                pipe.run(pe, step)

            @block.scalar
            def _(act):
                finish_stats(nc, act, g, "act", sems)
                act.wait_ge(s["loaded"], 32)
                nc.scalar.mul(gate_parts[:, 0], gate_raw[:, :, :], WS).then_inc(s["gate_hi"], 1)

                def step(r, j, live):
                    n = 4 * r + j
                    if live(HT):
                        u, slot = n - HT, (j - HT) % 4
                        act.wait_ge(s["h_t"], u + 1)
                        nc.scalar.copy(h_t[:, 0, :, bass.ds(u * P, P)],
                                       g.psum[:, slot, 0:D].rearrange("p (k n) -> p k n", k=KC)).then_inc(s["h_hi"], 1)
                    if live(LO):
                        u, slot = n - LO, (j - LO) % 4
                        act.wait_ge(s["logits"], u + 1)
                        nc.scalar.activation(scores[:, u, :], g.psum[:, 4 + slot, 0:NE], ACT.Sigmoid, scale=1.0 / WS).then_inc(s["logits_out"], 1)
                pipe.run(act, step)

            @block.vector
            def _(dve):
                finish_stats(nc, dve, g, "dve", sems)
                dve.wait_ge(sems[3], 1)
                dve.wait_ge(s["gate_hi"], 1)
                nc.vector.scalar_tensor_tensor(gate_parts[:, 1], gate_raw[:, :, :], WS, gate_parts[:, 0], ALU.mult,
                                               ALU.subtract).then_inc(s["gate_lo"], 1)

                def step(r, j, live):
                    n = 4 * r + j
                    if live(0):
                        u = n
                        wait(dve, s["h_t"], u - 3)
                        nc.vector.tensor_scalar(normed[:, j], res[:, u, :], g.mean[:, bass.ds(u, 1)], g.rstd[:, bass.ds(u, 1)],
                                                ALU.subtract, ALU.mult).then_inc(s["normed"], 1)
                    if live(HT):
                        u, slot = n - HT, (j - HT) % 4
                        dve.wait_ge(s["h_hi"], u + 1)
                        nc.vector.tensor_tensor(h_t[:, 1, :, bass.ds(u * P, P)], g.psum[:, slot, 0:D].rearrange("p (k n) -> p k n", k=KC),
                                                h_t[:, 0, :, bass.ds(u * P, P)], ALU.subtract).then_inc(s["h_lo"], 1)
                pipe.run(dve, step)

                nc.vector.memset(g.expert_w[:, 0:1, :], 1.0 / WS)
                dve.wait_ge(s["logits_out"], NT)
                chain = Chain(dve, s["steps"])
                tt = nc.vector.tensor_tensor
                chain(tt(choice[:, :, :], scores[:, :, :], bc(e_bias[:, :], 1, NT), ALU.add))
                quads = choice[:, :, :].rearrange("p t (g a b) -> p (t g) a b", a=2, b=2)
                high2 = high[:, :, :, :].rearrange("p t g a -> p (t g) a")
                low2 = low[:, :, :, :].rearrange("p t g a -> p (t g) a")
                sums = group_sum[:, :, :].rearrange("p t g -> p (t g)")
                seconds = second[:, :, :].rearrange("p t g -> p (t g)")
                chain(tt(high2, quads[:, :, :, 0], quads[:, :, :, 1], ALU.max))
                chain(tt(low2, quads[:, :, :, 0], quads[:, :, :, 1], ALU.min))
                chain(tt(sums, high2[:, :, 0], high2[:, :, 1], ALU.min))
                chain(tt(seconds, low2[:, :, 0], low2[:, :, 1], ALU.max))
                chain(tt(seconds, seconds, sums, ALU.max))
                chain(tt(sums, high2[:, :, 0], high2[:, :, 1], ALU.max))
                chain(tt(sums, sums, seconds, ALU.add))

                def ranks(out, values, n):
                    chain(nc.vector.memset(out, 0.0))
                    for e in range(n):
                        one = values[:, :, e:e + 1]
                        if e + 1 < n:
                            w = wins[:, :, e + 1:n]
                            chain(tt(w, one.to_broadcast([P, NT, n - 1 - e]), values[:, :, e + 1:n], ALU.is_ge))
                        if e:
                            chain(tt(wins[:, :, 0:e], one.to_broadcast([P, NT, e]), values[:, :, 0:e], ALU.is_gt))
                        chain(nc.vector.memset(wins[:, :, e:e + 1], 0.0))
                        chain(tt(out, out, wins[:, :, 0:n], ALU.add))
                ranks(group_rank[:, :, :], group_sum[:, :, :], GROUPS)
                chain(nc.vector.tensor_scalar(group_rank[:, :, :], group_rank[:, :, :], float(TOPK_GROUP), None, ALU.is_lt))
                by_group = choice[:, :, :].rearrange("p t (g a) -> p t g a", g=GROUPS)
                chain(tt(by_group, by_group, bc(group_rank[:, :, :], 3, PER_GROUP), ALU.mult))
                ranks(rank[:, :, :], choice[:, :, :], NE)
                chain(nc.vector.tensor_scalar(rank[:, :, :], rank[:, :, :], float(TOP_K), None, ALU.is_lt))
                chain(tt(scores[:, :, :], scores[:, :, :], rank[:, :, :], ALU.mult))
                chain(nc.vector.tensor_reduce(total[:, :], scores[:, :, :], AX.X, ALU.add))
                chain(nc.vector.tensor_scalar(total[:, :], total[:, :], 1e-20, None, ALU.add))
                chain(nc.vector.reciprocal(total[:, :], total[:, :]))
                chain(nc.vector.tensor_scalar(total[:, :], total[:, :], SCALING / WS, None, ALU.mult))
                tt(g.expert_w[:, 1:, :], scores[:, :, :].rearrange("p t e -> p e t"), bc(total[:, :], 1, NE), ALU.mult)


def moe(nc, g, io, res, h_t):
    WN = 2 * KC * INTER + D
    HALF = 2
    with Stage(nc, "moe") as st:
        raw = st.sb("raw", [P, 2, WN], F32)
        w = st.sb("w", [P, 2, 2, WN], F16)
        gated = st.sb("gated", [P, 2, S], F32)
        inner = st.sb("inner", [P, 2, S], F32)
        parts = st.sb("parts", [P, 2, 2, S], F16)
        raw_loaded = [st.sem(f"raw_loaded{n}") for n in range(2)]
        out_stored = st.sem("out_stored")
        s = {k: st.sem(k) for k in ("w_hi", "w_lo", "gate_up", "gated", "inner", "hi", "lo", "down", "summed")}

        def sweep(eng, chunk_step):
            def expert(x, slot):
                for j in range(HALF):
                    chunk_step(x, slot, 0, j)
                with eng.Fori(1, NC // HALF) as r:
                    for j in range(HALF):
                        chunk_step(x, slot, r, j)
            expert(0, 1)
            with eng.Fori(0, NE // 2 - 1) as pair:
                for e in range(2):
                    expert(pair * 2 + e + 1, e)
            for e in range(2):
                expert(NE - 1 + e, e)

        def static(x):
            return isinstance(x, int)

        with nc.Block() as block:
            @block.sync
            def _(sp):
                sp.dma_start(raw[:, 1], io["expert_cols"][0]).then_inc(raw_loaded[1], 16)
                sp.dma_start(raw[:, 0], io["expert_cols"][1]).then_inc(raw_loaded[0], 16)
                with sp.Fori(1, NE // 2) as pair:
                    for e in range(2):
                        x = pair * 2 + e
                        sp.wait_ge(s["w_lo"], x - 1)
                        sp.dma_start(raw[:, 1 - e], io["expert_cols"][x]).then_inc(raw_loaded[1 - e], 16)
                sp.wait_ge(s["w_lo"], NE - 1)
                sp.dma_start(raw[:, 1], io["expert_cols"][NE]).then_inc(raw_loaded[1], 16)
                with sp.Fori(0, NC) as c:
                    sp.wait_ge(s["summed"], (NC * NE + c + 1) * 2)
                    sp.dma_start(io["out"][c].rearrange("(t p) d -> p t d", p=P), res[:, bass.ds(c * TPB, TPB), :]).then_inc(out_stored, 16)
                sp.wait_ge(out_stored, 16 * NC)

            @block.tensor
            def _(pe):
                def down(u, slot, j):
                    pe.wait_ge(s["lo"], u + 1)
                    wait(pe, s["summed"], (u - 1) * 2)
                    for t in range(TPB):
                        bank = g.psum[:, 4 + 2 * j + t // 2, D * (t % 2):D * (t % 2 + 1)]
                        for i, (a, b) in enumerate(PASSES):
                            last = nc.tensor.matmul(bank, parts[:, j, a, P * t:P * (t + 1)], w[:, slot, b, 2 * KC * INTER:],
                                                    start=(i == 0), stop=(i == 2))
                        if t % 2:
                            last.then_inc(s["down"], 1)

                def chunk_step(x, slot, r, j):
                    u = NC * x + HALF * r + j
                    first = static(r) and j == 0
                    if first:
                        pe.wait_ge(s["w_lo"], x + 1)
                    wait(pe, s["inner"], u - 1)
                    for q in range(2):
                        for k in range(KC):
                            at = INTER * (KC * q + k)
                            for i, (a, b) in enumerate(PASSES):
                                last = nc.tensor.matmul(g.psum[:, 2 * j + q, :], w[:, slot, a, at:at + INTER],
                                                        h_t[:, b, k, bass.ds((HALF * r + j) * S, S)],
                                                        start=(k == 0 and i == 0), stop=(k == KC - 1 and i == 2))
                    last.then_inc(s["gate_up"], 1)
                    if not (first and static(x) and x == 0):
                        down(u - 1, 1 - slot if first else slot, 1 - j)
                sweep(pe, chunk_step)
                down(NC * (NE + 1) - 1, 1, 1)

            @block.scalar
            def _(act):
                def split(x, slot):
                    act.wait_ge(raw_loaded[slot], (x - (1 - slot)) * 8 + 16)
                    wait(act, s["down"], NC * (x - 1) * 2)
                    nc.scalar.mul(w[:, slot, 0], raw[:, slot], WS).then_inc(s["w_hi"], 1)
                split(0, 1)

                def chunk_step(x, slot, r, j):
                    u = NC * x + HALF * r + j
                    act.wait_ge(s["gate_up"], u + 1)
                    wait(act, s["inner"], u - 1)
                    nc.scalar.activation(gated[:, j], g.psum[:, 2 * j, :], ACT.Silu, scale=1.0 / WS).then_inc(s["gated"], 1)
                    act.wait_ge(s["inner"], u + 1)
                    wait(act, s["down"], 2 * (u - 1))
                    nc.scalar.copy(parts[:, j, 0], inner[:, j]).then_inc(s["hi"], 1)
                    if static(r) and j == 1 and not (static(x) and x == NE):
                        split(x + 1, 1 - slot)
                sweep(act, chunk_step)

            @block.vector
            def _(dve):
                def split(x, slot):
                    dve.wait_ge(s["w_hi"], x + 1)
                    nc.vector.scalar_tensor_tensor(w[:, slot, 1], raw[:, slot], WS, w[:, slot, 0], ALU.mult,
                                                   ALU.subtract).then_inc(s["w_lo"], 1)
                split(0, 1)

                def gather(x, u, c, j):
                    if not (static(x) and x == 0):
                        dve.wait_ge(s["summed"], 2 * (u - NC + 1))
                    for t in range(TPB):
                        if t % 2 == 0:
                            dve.wait_ge(s["down"], 2 * u + t // 2 + 1)
                        tile = c * TPB + t
                        weight = g.expert_w[:, x, bass.ds(tile, 1)]
                        last = nc.vector.scalar_tensor_tensor(res[:, tile, :], g.psum[:, 4 + 2 * j + t // 2, D * (t % 2):D * (t % 2 + 1)],
                                                              weight, res[:, tile, :], ALU.mult, ALU.add)
                        if t % 2:
                            last.then_inc(s["summed"], 1)

                def chunk_step(x, slot, r, j):
                    u = NC * x + HALF * r + j
                    dve.wait_ge(s["gated"], u + 1)
                    wait(dve, s["lo"], u - 1)
                    nc.vector.scalar_tensor_tensor(inner[:, j], g.psum[:, 2 * j + 1, :], 1.0 / WS, gated[:, j], ALU.mult,
                                                   ALU.mult).then_inc(s["inner"], 1)
                    dve.wait_ge(s["inner"], u + 1)
                    dve.wait_ge(s["hi"], u + 1)
                    nc.vector.tensor_tensor(parts[:, j, 1], inner[:, j], parts[:, j, 0], ALU.subtract).then_inc(s["lo"], 1)
                    if not (static(r) and j == 0):
                        gather(x, u - 1, HALF * r + j - 1, 1 - j)
                    elif not (static(x) and x == 0):
                        gather(x - 1, u - 1, NC - 1, 1 - j)
                    if static(r) and j == 1 and not (static(x) and x == NE):
                        split(x + 1, 1 - slot)
                sweep(dve, chunk_step)
                gather(NE, NC * (NE + 1) - 1, NC - 1, 1)


class Shared:
    pass


def build(nc, io, upto=99):
    Stage.cleared = []
    with ExitStack() as ctx:
        def sb(name, shape, dt):
            return ctx.enter_context(nc.sbuf_tensor(name, shape, dt))
        g = Shared()
        g.psum = ctx.enter_context(nc.psum_tensor("psum", [P, 8, 512], F32))
        g.ident32 = sb("ident32", [P, P], F32)
        g.ident16 = sb("ident16", [P, P], F16)
        g.identb = sb("identb", [P, P], BF16)
        g.head_mask = sb("head_mask", [P, HPP, KEYS], F16)
        g.stats = sb("stats", [P, NT, 6], F32)
        g.mean = sb("mean", [P, NT], F32)
        g.var = sb("var", [P, NT], F32)
        g.rstd = sb("rstd", [P, NT], F32)
        g.out_bias = sb("out_bias", [P, D], F32)
        g.q_bias = sb("q_bias", [P, KC], F32)
        wq = sb("wq", [P, 2, KC, D], F16)
        wo = sb("wo", [P, 2, KC, D], F16)
        g.scal = sb("scal", [P, 16], F32)
        g.res = sb("res", [P, NT, D], F32)
        wide = sb("wide", [P, NT * 2 * KC * P], F16)
        constants(nc, g)
        wide_rows = wide[:, :].bitcast(F32).rearrange("p (t d) -> p t d", d=D)
        res_words = g.res[:, :, :].rearrange("p t d -> p (t d)")
        shape = dict(a=2, b=B, m=KC, h=HPP)

        def attend(layer, res, kbd):
            with nc.sbuf_tensor(f"values{layer}", [P, B, PAIRS, 2 * VC], F32) as vbd:
                attention_prep(nc, g, io, layer, kbd, vbd, wq, wo)
                attention(nc, g, io, layer, res, kbd.rearrange("p a b m h k -> p a b m (h k)"), vbd, wq, wo)

        attend(0, g.res, wide[:, :].rearrange("p (a b m h k) -> p a b m h k", **shape))
        h_parts_t = wide[:, :].rearrange("p (a k n) -> p a k n", a=2, k=KC)
        with Stage(nc, "ffn") as st:
            w_d = st.sb("w_d", [P, 2, NI, D], F16)
            tail = st.sb("gate_tail", [P, 2, B * S], I16)
            front = res_words.bitcast(I16).rearrange("p (i n) -> p i n", i=NI - 2)

            def gate_int(n):
                return front[:, 2 * n:2 * n + 2, :] if n < PAIR_I - 1 else tail[:, :, :]
            with nc.sbuf_tensor("w_gu", [P, 2, 2, KC, FF], F16) as w_gu:
                ffn_prep(nc, g, io, w_gu, w_d, h_parts_t, tail[:, :, :].rearrange("p i n -> p (i n)"))
                ffn_peaks(nc, g, w_gu, h_parts_t)
                ffn_gate(nc, g, w_gu, h_parts_t, gate_int)
                ffn_up(nc, g, io, w_gu, h_parts_t, gate_int)
            ffn_down(nc, g, io, w_d, gate_int, wide_rows)
        if upto == 2:
            return dump(nc, io, wide_rows)
        attend(1, wide_rows, res_words.bitcast(F16).rearrange("p (a b m h k) -> p a b m h k", **shape))
        if upto == 3:
            return dump(nc, io, wide_rows)
        with nc.sbuf_tensor("expert_w", [P, NE + 1, NT], F32) as g.expert_w:
            h_t = res_words.bitcast(F16).rearrange("p (a k n) -> p a k n", a=2, k=KC)
            moe_prep(nc, g, io, wide_rows, h_t)
            moe(nc, g, io, wide_rows, h_t)


def dump(nc, io, rows):
    with nc.semaphore("dumped") as sem, nc.Block() as block:
        @block.sync
        def _(sp):
            sp.dma_start(io["dbg"], rows).then_inc(sem, 16)
            sp.wait_ge(sem, 16)


def arrays_of(inputs):
    import numpy as np
    a = {k: np.asarray(v) for k, v in inputs.items()}
    ctx = a["ctx_1024"]
    out = {
        "x": a["x"], "ctx": ctx, "ctx_T": ctx.transpose(2, 0, 1).reshape(D, B * KEYS),
        "mask0": a["mask_Bx1xSxS2_fk0"].reshape(B * S, KEYS), "mask1": a["mask_Bx1xSxS2_ik1"].reshape(B * S, KEYS),
        "L1_xattn_WoT": a["L1_xattn_Wo"].T,
    }
    for k in ("Wq", "bq", "Wk", "bk", "Wv", "bv", "Wo", "bo"):
        out[f"L0_xattn_{k}"] = a[f"L0_xattn_{k}"]
    for k in ("w_gate", "w_up", "w_down"):
        out[f"L0_ffn_{k}"] = a[f"L0_ffn_{k}"]
    gates = np.concatenate([a["L1_ffn_shared_gate_w"][None], a["L1_ffn_gate_proj"]])
    ups = np.concatenate([a["L1_ffn_shared_up_w"][None], a["L1_ffn_up_proj"]])
    downs = np.concatenate([a["L1_ffn_shared_down_w"][None], a["L1_ffn_down_proj"]])
    ins = np.stack([gates, ups], 1).reshape(NE + 1, 2, INTER, KC, P).transpose(0, 4, 1, 3, 2)
    out["expert_cols"] = np.concatenate([ins.reshape(NE + 1, P, 2 * KC * INTER), downs.transpose(0, 2, 1)], 2)
    out["moe_gate_T"] = a["L1_ffn_gate_w"].T
    out["moe_e_bias"] = a["L1_ffn_e_bias"]
    out["L1_xattn_bo"] = a["L1_xattn_bo"]
    return {k: np.ascontiguousarray(v) for k, v in out.items()}


def program(nc, arrays, upto=99):
    io = {k: nc.dram_tensor(k, v.shape, mybir.dt.from_np(v.dtype), kind="ExternalInput").ap() for k, v in arrays.items()}
    io["x1_spill"] = nc.dram_tensor("x1_spill", (P, B, TPB, D), F32, kind="Internal").ap()
    io["up_spill"] = nc.dram_tensor("up_spill", (P, NC, PAIR_I, 2, S), I16, kind="Internal").ap()
    if upto != 99:
        io["dbg"] = nc.dram_tensor("dbg", (P, NT, D), F32, kind="ExternalOutput").ap()
    io["out"] = nc.dram_tensor("out", (B, S, D), F32, kind="ExternalOutput").ap()
    build(nc, io, upto)


def kernel(**inputs):
    import concourse.bacc as bacc
    from concourse.bass_utils import run_bass_kernel_spmd as run
    nc = bacc.Bacc("TRN2", target_bir_lowering=False, num_devices=1)
    arrays = arrays_of(inputs)
    program(nc, arrays)
    return run(nc, [arrays], core_ids=[0]).results[0]["out"]
```

```python
from contextlib import ExitStack

import concourse.bass as bass
from concourse import mybir

P = 128
F32, F16, BF16 = mybir.dt.float32, mybir.dt.float16, mybir.dt.bfloat16
I32, I16, U16 = mybir.dt.int32, mybir.dt.int16, mybir.dt.uint16
ALU, ACT, AX = mybir.AluOpType, mybir.ActivationFunctionType, mybir.AxisListType
RMAX = bass.bass_isa.ReduceOp.max

B, S, D = 16, 512, 256
KEYS, HEADS, HD = 64, 16, 16
NT = B * S // P
TPB = S // P
KC = D // P
HPP = P // HD
PAIRS = HEADS // 2
VC = HD + 1
FF = 768
NI = FF // P
QB = 32
NE, INTER = 16, 128
GROUPS, PER_GROUP, TOPK_GROUP, TOP_K, SCALING = 4, 4, 2, 4, 2.5
WS = 64.0
QMAX = 32767.0
EPS = 1e-5
PASSES = ((0, 0), (0, 1), (1, 0))


def bc(ap, axis, n):
    a = ap.unsqueeze(axis)
    shape = list(a.shape)
    shape[axis] = n
    return a.to_broadcast(shape)


class Tiles:

    def __init__(self, count, unroll, lead, depth):
        self.count, self.unroll, self.lead, self.depth = count, unroll, lead, depth

    def run(self, eng, step):
        for n in range(self.lead):
            step(n // self.unroll, n % self.unroll, lambda lag, n=n: 0 <= n - lag < self.count)
        with eng.Fori(self.lead // self.unroll, self.count // self.unroll) as r:
            for j in range(self.unroll):
                step(r, j, lambda lag: True)
        for n in range(self.count, self.count + self.depth):
            step(n // self.unroll, n % self.unroll, lambda lag, n=n: 0 <= n - lag < self.count)


def since(value, least=1):
    return not isinstance(value, int) or value >= least


def wait(eng, sem, value):
    if since(value):
        eng.wait_ge(sem, value)


class Chain:

    def __init__(self, eng, sem):
        self.eng, self.sem, self.n = eng, sem, 0

    def __call__(self, ins):
        self.n += 1
        ins.then_inc(self.sem, 1)
        self.eng.wait_ge(self.sem, self.n)


class Stage:
    cleared = []

    def __init__(self, nc, name):
        self.nc, self.name, self.ctx, self.sems = nc, name, ExitStack(), []

    def __enter__(self):
        self.ctx.__enter__()
        return self

    def __exit__(self, *a):
        for sem in self.sems:
            self.nc.gpsimd.sem_clear(sem)
        for sem in Stage.cleared:
            self.nc.release_semaphore(sem)
        Stage.cleared = self.sems
        return self.ctx.__exit__(*a)

    def sb(self, name, shape, dt):
        return self.ctx.enter_context(self.nc.sbuf_tensor(f"{self.name}_{name}", shape, dt))

    def sem(self, name):
        self.sems.append(self.nc.alloc_semaphore(f"{self.name}_{name}"))
        return self.sems[-1]


def constants(nc, g):
    with Stage(nc, "const") as st:
        zeroed = st.sem("zeroed")
        written = st.sem("written")
        with nc.Block() as block:
            @block.gpsimd
            def _(pool):
                nc.gpsimd.memset(g.ident32[:, :], 0.0).then_inc(zeroed, 1)
                nc.gpsimd.memset(g.head_mask[:, :, :], 1.0).then_inc(zeroed, 1)
                pool.wait_ge(zeroed, 2)
                nc.gpsimd.affine_select(out=g.ident32[:, :], in_=g.ident32[:, :], compare_op=ALU.not_equal,
                                        fill=1.0, base=0, pattern=[[-1, P]], channel_multiplier=1).then_inc(written, 1)
                nc.gpsimd.affine_select(out=g.head_mask[:, :, :], in_=g.head_mask[:, :, :], compare_op=ALU.is_ge,
                                        fill=0.0, base=0, pattern=[[-HD, HPP], [0, KEYS]],
                                        channel_multiplier=1).then_inc(written, 1)
                pool.wait_ge(written, 2)
                nc.gpsimd.affine_select(out=g.head_mask[:, :, :], in_=g.head_mask[:, :, :], compare_op=ALU.is_ge,
                                        fill=0.0, base=HD - 1, pattern=[[HD, HPP], [0, KEYS]],
                                        channel_multiplier=-1).then_inc(written, 1)

            @block.vector
            def _(dve):
                dve.wait_ge(written, 1)
                nc.vector.tensor_copy(g.ident16[:, :], g.ident32[:, :])
                nc.vector.tensor_copy(g.identb[:, :], g.ident32[:, :])


def finish_stats(nc, eng, g, side, sems):
    steps, var_ready, std_ready, done = sems
    if side == "act":
        eng.wait_ge(var_ready, 1)
        nc.scalar.activation(g.rstd[:, :], g.var[:, :], ACT.Sqrt).then_inc(std_ready, 1)
        return
    chain = Chain(eng, steps)
    even_m, even_v = g.stats[:, :, 1], g.stats[:, :, 2]
    odd_m, odd_v = g.stats[:, :, 4], g.stats[:, :, 5]
    chain(nc.vector.tensor_tensor(g.mean[:, :], even_m, odd_m, ALU.add))
    chain(nc.vector.tensor_scalar(g.mean[:, :], g.mean[:, :], 0.5, None, ALU.mult))
    chain(nc.vector.tensor_tensor(g.var[:, :], even_m, odd_m, ALU.subtract))
    chain(nc.vector.tensor_tensor(g.var[:, :], g.var[:, :], g.var[:, :], ALU.mult))
    chain(nc.vector.tensor_scalar(g.var[:, :], g.var[:, :], 0.25, EPS, ALU.mult, ALU.add))
    chain(nc.vector.tensor_tensor(g.rstd[:, :], even_v, odd_v, ALU.add))
    chain(nc.vector.tensor_scalar(g.rstd[:, :], g.rstd[:, :], 1.0 / D, None, ALU.mult))
    nc.vector.tensor_tensor(g.var[:, :], g.var[:, :], g.rstd[:, :], ALU.add).then_inc(var_ready, 1)
    eng.wait_ge(std_ready, 1)
    chain(nc.vector.reciprocal(g.rstd[:, :], g.rstd[:, :]))
    nc.vector.scalar_tensor_tensor(g.shift[:, :], g.mean[:, :], -1.0, g.rstd[:, :], ALU.mult, ALU.mult).then_inc(done, 1)


def attention_prep(nc, g, io, layer, kbd, vbd, wq, wo):
    with Stage(nc, f"prep{layer}") as st:
        ctx_t = st.sb("ctx_t", [P, KC, B * KEYS], F32)
        ctx_parts = st.sb("ctx_parts", [P, 2, KC, B * KEYS], F16)
        w_raw = st.sb("w_raw", [P, 4, KC, D], F32)
        loaded = {k: st.sem(f"loaded_{k}") for k in ("ctx", "w", "bias", "ctx_dup")}
        x_loaded = [st.sem(f"x_loaded{b}") for b in range(B if layer == 0 else 0)]
        split_hi, split_lo = st.sem("split_hi"), st.sem("split_lo")
        zeroed, ones_set = st.sem("zeroed"), st.sem("ones_set")
        k_product, k_hi, k_lo = st.sem("k_product"), st.sem("k_hi"), st.sem("k_lo")
        v_product, v_stored = st.sem("v_product"), st.sem("v_stored")
        stats_done = st.sem("stats_done")
        out_bias = st.sb("out_bias", [1, D], F32)
        bias_low = st.sb("bias_low", [1, D], F16)
        bias_loaded, bias_zeroed, bias_hi = st.sem("bias_loaded"), st.sem("bias_zeroed"), st.sem("bias_hi")
        bias_lo, bias_placed = st.sem("bias_lo"), st.sem("bias_placed")
        sems = (st.sem("stat_steps"), st.sem("var_ready"), st.sem("std_ready"), st.sem("rstd_ready"))
        ps = g.psum
        if layer == 0:
            wkv = st.sb("wkv", [P, 2, 2, KC, D], F16)
            v_bias = st.sb("v_bias", [P, PAIRS, HD], F32)
            q_bias_raw = st.sb("q_bias_raw", [P, KC], F32)
            key_bias = st.sb("key_bias", [P, KC], F32)
            k_parts = st.sb("k_parts", [P, 2, KC, B * KEYS], F16)
            names = ["L0_xattn_Wq", "L0_xattn_Wo", "L0_xattn_Wk", "L0_xattn_Wv"]
            targets = [wq, wo, wkv[:, 0], wkv[:, 1]]
        else:
            ctx_dup = st.sb("ctx_dup", [P, B, D], F32)
            k_parts = ctx_parts
            names = ["L1_xattn_WoT"]
            targets = [wo]
        NW = len(names)
        with nc.Block() as block:
            @block.sync
            def _(sp):
                sp.dma_start(ctx_t[:, :, :], io["ctx_T"].rearrange("(k p) n -> p k n", p=P)).then_inc(loaded["ctx"], 16)
                for n, name in enumerate(names):
                    sp.dma_start(w_raw[:, n], io[name].rearrange("(k p) n -> p k n", p=P)).then_inc(loaded["w"], 16)
                sp.dma_start(out_bias[:, :], io[f"L{layer}_xattn_bo"].rearrange("(a n) -> a n", a=1)).then_inc(bias_loaded, 16)
                sp.wait_ge(bias_lo, 1)
                sp.dma_start(g.bias_rows[1:2, :], bias_low[:, :]).then_inc(bias_placed, 16)
                if layer == 0:
                    sp.dma_start(q_bias_raw[:, :], io["L0_xattn_bq"].rearrange("(k p) -> p k", p=P), allow_slow_non_contiguous=True).then_inc(loaded["bias"], 16)
                    sp.dma_start(key_bias[:, :], io["L0_xattn_bk"].rearrange("(k p) -> p k", p=P), allow_slow_non_contiguous=True).then_inc(loaded["bias"], 16)
                    bv = io["L0_xattn_bv"].rearrange("(p e d) -> e p d", e=2, d=HD)
                    for e in range(2):
                        sp.dma_start(v_bias[KEYS * e:KEYS * (e + 1)],
                                     bv[e:e + 1].to_broadcast([KEYS, PAIRS, HD])).then_inc(loaded["bias"], 16)
                    for b in range(B):
                        sp.dma_start(g.res[:, TPB * b:TPB * (b + 1), :],
                                     io["x"][b].rearrange("(t p) d -> p t d", p=P)).then_inc(x_loaded[b], 16)
                else:
                    for e in range(2):
                        sp.dma_start(ctx_dup[KEYS * e:KEYS * (e + 1)],
                                     io["ctx"].rearrange("b k d -> k b d")).then_inc(loaded["ctx_dup"], 16)
                sp.wait_ge(bias_placed, 16)

            @block.gpsimd
            def _(pool):
                nc.gpsimd.memset(g.ones_rows[:, :], 1.0)
                nc.gpsimd.memset(g.bias_rows[:, :], 0.0).then_inc(bias_zeroed, 1)
                nc.gpsimd.memset(vbd[:, :, :, :], 0.0).then_inc(zeroed, 1)
                pool.wait_ge(zeroed, 1)
                for e in range(2):
                    col = e * VC + HD
                    nc.gpsimd.memset(vbd[KEYS * e:KEYS * (e + 1), :, :, col:col + 1], 1.0).then_inc(ones_set, 1)

            @block.scalar
            def _(act):
                act.wait_ge(loaded["ctx"], 16)
                nc.scalar.copy(ctx_parts[:, 0], ctx_t[:, :, :]).then_inc(split_hi, 1)
                for n in range(NW):
                    act.wait_ge(loaded["w"], 16 * NW)
                    nc.scalar.mul(targets[n][:, 0], w_raw[:, n], WS).then_inc(split_hi, 1)
                if layer == 0:
                    for h in range(KC):
                        for c in range(2):
                            n = 2 * h + c
                            act.wait_ge(k_product, n + 1)
                            act.wait_ge(loaded["bias"], 16 * 4)
                            nc.scalar.activation(k_parts[:, 0, h, 512 * c:512 * (c + 1)], ps[:, n], ACT.Identity,
                                                 bias=key_bias[:, h:h + 1], scale=1.0 / WS).then_inc(k_hi, 1)
                finish_stats(nc, act, g, "act", sems)

            @block.tensor
            def _(pe):
                if layer:
                    return
                pe.wait_ge(split_lo, 1 + NW)
                for h in range(KC):
                    for c in range(2):
                        for k in range(KC):
                            for i, (a, b) in enumerate(PASSES):
                                last = nc.tensor.matmul(ps[:, 2 * h + c], wkv[:, 0, a, k, P * h:P * (h + 1)],
                                                        ctx_parts[:, b, k, 512 * c:512 * (c + 1)],
                                                        start=(k == 0 and i == 0), stop=(k == KC - 1 and i == 2))
                        last.then_inc(k_product, 1)
                for b in range(B):
                    if b >= 4:
                        pe.wait_ge(v_stored, 2 * (b - 3))
                    for e in range(2):
                        for k in range(KC):
                            w = [wkv[:, 1, i, k, :].rearrange("c (p e d) -> c e p d", e=2, d=HD)[:, e] for i in range(2)]
                            for i, (a, m) in enumerate(PASSES):
                                last = nc.tensor.matmul(ps[KEYS * e:KEYS * (e + 1), 4 + b % 4, 0:PAIRS * HD],
                                                        ctx_parts[:, a, k, KEYS * b:KEYS * (b + 1)], w[m],
                                                        start=(k == 0 and i == 0), stop=(k == KC - 1 and i == 2))
                    last.then_inc(v_product, 1)

            @block.vector
            def _(dve):
                dve.wait_ge(bias_loaded, 16)
                dve.wait_ge(bias_zeroed, 1)
                nc.vector.tensor_scalar(g.bias_rows[0:1, :], out_bias[:, :], WS, None, ALU.mult).then_inc(bias_hi, 1)
                dve.wait_ge(bias_hi, 1)
                nc.vector.scalar_tensor_tensor(bias_low[:, :], out_bias[:, :], WS, g.bias_rows[0:1, :], ALU.mult,
                                               ALU.subtract).then_inc(bias_lo, 1)
                if layer == 0:
                    dve.wait_ge(loaded["bias"], 16 * 4)
                    nc.vector.tensor_scalar(g.q_bias[:, :], q_bias_raw[:, :], WS, None, ALU.mult)
                dve.wait_ge(split_hi, 1)
                nc.vector.tensor_tensor(ctx_parts[:, 1], ctx_t[:, :, :], ctx_parts[:, 0], ALU.subtract).then_inc(split_lo, 1)
                for n in range(NW):
                    dve.wait_ge(split_hi, n + 2)
                    nc.vector.scalar_tensor_tensor(targets[n][:, 1], w_raw[:, n], WS, targets[n][:, 0],
                                                   ALU.mult, ALU.subtract).then_inc(split_lo, 1)
                if layer == 0:
                    dve.wait_ge(loaded["bias"], 16 * 4)
                    for n in range(2 * KC):
                        h, c = n // 2, n % 2
                        dve.wait_ge(k_hi, n + 1)
                        raw = w_raw[:, n, :, :].rearrange("p k n -> p (k n)")
                        nc.vector.tensor_scalar(raw, ps[:, n], 1.0 / WS, key_bias[:, h:h + 1], ALU.mult, ALU.add).then_inc(k_lo, 1)
                        dve.wait_ge(k_lo, 2 * n + 1)
                        nc.vector.tensor_tensor(k_parts[:, 1, h, 512 * c:512 * (c + 1)], raw,
                                                k_parts[:, 0, h, 512 * c:512 * (c + 1)], ALU.subtract).then_inc(k_lo, 1)
                    dve.wait_ge(k_lo, 4 * KC)
                else:
                    dve.wait_ge(split_lo, 1)
                for part in range(2):
                    for h in range(KC):
                        keys = bc(k_parts[:, part, h, :].rearrange("p (b k) -> p b k", b=B), 2, HPP)
                        nc.vector.tensor_tensor(kbd[:, part, :, h], keys, bc(g.head_mask[:, :, :], 1, B), ALU.mult)
                dve.wait_ge(ones_set, 2)
                if layer == 0:
                    for b in range(B):
                        dve.wait_ge(v_product, b + 1)
                        for e in range(2):
                            rows = slice(KEYS * e, KEYS * (e + 1))
                            nc.vector.scalar_tensor_tensor(
                                vbd[rows, b, :, VC * e:VC * e + HD],
                                ps[rows, 4 + b % 4, 0:PAIRS * HD].rearrange("p (a d) -> p a d", d=HD), 1.0 / WS,
                                v_bias[rows], ALU.mult, ALU.add).then_inc(v_stored, 1)
                    for b in range(B):
                        dve.wait_ge(x_loaded[b], 16)
                        for t in range(TPB):
                            last = nc.vector.bn_stats(g.stats[:, TPB * b + t, :], g.res[:, TPB * b + t, :])
                    last.then_inc(stats_done, 1)
                    dve.wait_ge(stats_done, 1)
                else:
                    dve.wait_ge(loaded["ctx_dup"], 32)
                    for e in range(2):
                        rows = slice(KEYS * e, KEYS * (e + 1))
                        nc.vector.tensor_copy(vbd[rows, :, :, VC * e:VC * e + HD],
                                              ctx_dup[rows].rearrange("p b (a e d) -> p b e a d", e=2, d=HD)[:, :, e])
                finish_stats(nc, dve, g, "dve", sems)


def attention(nc, g, io, layer, res, kbd, vbd, wq, wo):
    LN, HT, QP, SC, MX, EX, PT, AV, OT, OUT, RES = range(11)
    pipe = Tiles(NT, TPB, 12, RES)
    with Stage(nc, f"attn{layer}") as st:
        normed = st.sb("normed", [P, 2, D], F32)
        h_parts = st.sb("h_parts", [P, 4, 2, KC, P], F16)
        probs = st.sb("probs", [P, 4, HEADS, KEYS], F32)
        probs_t = st.sb("probs_t", [P, 2, PAIRS, P], F32)
        row_max = st.sb("row_max", [P, 4, HEADS], F32)
        row_sum = st.sb("row_sum", [P, 2, HEADS], F32)
        heads_out = st.sb("heads_out", [P, 2, D], F32)
        o_parts = st.sb("o_parts", [P, 2, 2, KC, P], F16)
        if layer == 0:
            q_parts = st.sb("q_parts", [P, 2, 2, KC, P], F16)
            fill = st.sb("fill", [P, HEADS, KEYS], F32)
            mask = st.sb("mask", [P, TPB, KEYS], F32)
        else:
            mask = st.sb("mask", [P, TPB, KEYS], I32)
            mask_fill = st.sb("mask_fill", [P, TPB, KEYS], BF16)
        mask_loaded = [st.sem(f"mask_loaded{t}") for t in range(TPB)]
        s = {k: st.sem(k) for k in (
            "normed", "h_t", "h_hi", "h_lo", "q", "q_hi", "q_lo", "scores", "mask_used", "fill", "filled", "max",
            "shifted", "exp", "p_t", "p_t_out", "av", "recip", "heads", "o_t", "o_hi", "o_lo", "projected",
            "residual", "stored", "held")}
        ps = g.psum
        ps_h = ps[:, 0, 0:D].rearrange("p (k n) -> p k n", k=KC)
        ps_q = ps[:, 7, 0:D].rearrange("p (k n) -> p k n", k=KC)
        ps_s = ps[:, 1:3, :].rearrange("p a (h k) -> p (a h) k", k=KEYS)
        ps_p = ps[:, 3:5, :].rearrange("p a (r q) -> p (a r) q", q=P)
        ps_v = ps[:, 5, 0:PAIRS * 2 * VC].rearrange("p (h c) -> p h c", c=VC)
        ps_o = ps[:, 6, 0:D].rearrange("p (k n) -> p k n", k=KC)
        ps_y = ps[:, 6, D:2 * D] if layer == 0 else ps[:, 7, 0:D]
        exp_scale = 0.25 / WS if layer == 0 else 1.0 / 16.0
        with nc.Block() as block:
            @block.sync
            def _(sp):
                by_tile = io[f"mask{layer}"].rearrange("(t p) k -> t p k", p=P)
                for t in range(TPB):
                    sp.dma_start(mask[:, t], by_tile[t]).then_inc(mask_loaded[t], 16)
                LATE = -(-RES // TPB) + 1

                def load_masks(c):
                    for t in range(TPB):
                        sp.wait_ge(s["mask_used" if layer == 0 else "fill"], (c - 1) * TPB + t + 1)
                        sp.dma_start(mask[:, t], by_tile[c * TPB + t]).then_inc(mask_loaded[t], 16)

                def spill(c):
                    sp.wait_ge(s["residual"], (c + 1) * TPB)
                    sp.dma_start(io["x1_spill"][:, c], res[:, bass.ds(c * TPB, TPB), :]).then_inc(s["stored"], 16)
                for c in range(1, LATE):
                    load_masks(c)
                with sp.Fori(LATE, B) as c:
                    load_masks(c)
                    if layer == 0:
                        spill(c - LATE)
                if layer == 0:
                    for c in range(B - LATE, B):
                        spill(c)
                    sp.wait_ge(s["stored"], 16 * B)

            @block.gpsimd
            def _(pool):
                def step(r, j, live):
                    n = TPB * r + j
                    if live(MX):
                        u, slot = n - MX, (j - MX) % 4
                        pool.wait_ge(s["max"], u + 1)
                        nc.gpsimd.tensor_tensor(probs[:, slot], probs[:, slot], bc(row_max[:, slot], 2, KEYS),
                                                ALU.subtract).then_inc(s["shifted"], 1)
                    if live(SC):
                        u, slot = n - SC, (j - SC) % 4
                        pool.wait_ge(s["fill"], u + 1)
                        nc.gpsimd.tensor_tensor(probs[:, slot], probs[:, slot], fill[:, :, :], ALU.add).then_inc(s["filled"], 1)
                if layer == 0:
                    pipe.run(pool, step)

            @block.tensor
            def _(pe):
                def step(r, j, live):
                    n = TPB * r + j
                    if live(HT):
                        u, slot = n - HT, (j - HT) % 2
                        pe.wait_ge(s["normed"], u + 1)
                        wait(pe, s["h_lo"], u)
                        for k in range(KC):
                            last = nc.tensor.transpose(ps_h[:, k], normed[:, slot, P * k:P * (k + 1)], g.ident32[:, :])
                        last.then_inc(s["h_t"], 1)
                    if layer == 0 and live(QP):
                        u = n - QP
                        pe.wait_ge(s["h_lo"], u + 1)
                        wait(pe, s["q_lo"], u)
                        for m in range(KC):
                            for k in range(KC):
                                for i, (a, b) in enumerate(PASSES):
                                    last = nc.tensor.matmul(ps_q[:, m], wq[:, a, k, P * m:P * (m + 1)],
                                                            h_parts[:, (j - QP) % 4, b, k], start=(k == 0 and i == 0),
                                                            stop=(k == KC - 1 and i == 2))
                        last.then_inc(s["q"], 1)
                    if live(OT):
                        u, slot = n - OT, (j - OT) % 2
                        pe.wait_ge(s["heads"], u + 1)
                        wait(pe, s["o_lo"], u)
                        if layer == 0:
                            wait(pe, s["residual"], u - 1)
                        for k in range(KC):
                            last = nc.tensor.transpose(ps_o[:, k], heads_out[:, slot, P * k:P * (k + 1)], g.ident32[:, :])
                        last.then_inc(s["o_t"], 1)
                    if live(SC):
                        u = n - SC
                        batch = r + (j - SC) // TPB
                        pe.wait_ge(s["q_lo" if layer == 0 else "h_lo"], u + 1)
                        wait(pe, s["mask_used" if layer == 0 else "shifted"], u)
                        q = q_parts[:, (j - SC) % 2] if layer == 0 else h_parts[:, (j - SC) % 4]
                        for m in range(KC):
                            out = ps[:, 1 + m, :]
                            if layer == 1:
                                pe.wait_ge(s["fill"], u + 1)
                                nc.tensor.matmul(out, g.identb[:, :], bc(mask_fill[:, (j - SC) % 4], 1, HPP), start=True, stop=False)
                            for i, (a, b) in enumerate(PASSES):
                                last = nc.tensor.matmul(out, q[:, a, m], kbd[:, b, batch, m],
                                                        start=(layer == 0 and i == 0), stop=(i == 2))
                        last.then_inc(s["scores"], 1)
                    if live(PT):
                        u, slot = n - PT, (j - PT) % 4
                        pe.wait_ge(s["exp"], u + 1)
                        for half in range(2):
                            wait(pe, s["p_t_out"], 2 * u + half - 1)
                            for a in range(PAIRS // 2 * half, PAIRS // 2 * (half + 1)):
                                pair = probs[:, slot, 2 * a:2 * a + 2, :].rearrange("p h k -> p (h k)")
                                last = nc.tensor.transpose(ps_p[:, a], pair, g.ident32[:, :])
                            last.then_inc(s["p_t"], 1)
                    if live(AV):
                        u, slot = n - AV, (j - AV) % 2
                        batch = r + (j - AV) // TPB
                        pe.wait_ge(s["p_t_out"], 2 * u + 2)
                        wait(pe, s["heads"], u)
                        for a in range(PAIRS):
                            last = nc.tensor.matmul(ps_v[:, 2 * a:2 * a + 2, :].rearrange("p h c -> p (h c)"),
                                                    probs_t[:, slot, a], vbd[:, batch, a], start=True, stop=True)
                        last.then_inc(s["av"], 1)
                    if live(OUT):
                        u, slot = n - OUT, (j - OUT) % 2
                        pe.wait_ge(s["o_lo"], u + 2 if layer == 0 and live(OT) else u + 1)
                        if layer == 1 or not live(OT):
                            wait(pe, s["residual"], u)
                        nc.tensor.matmul(ps_y, g.ones_rows[:, :], g.bias_rows[:, :], start=True, stop=False)
                        for k in range(KC):
                            for i, (a, b) in enumerate(PASSES):
                                last = nc.tensor.matmul(ps_y, o_parts[:, slot, a, k], wo[:, b, k],
                                                        start=False, stop=(k == KC - 1 and i == 2))
                        last.then_inc(s["projected"], 1)
                pipe.run(pe, step)

            @block.scalar
            def _(act):
                def step(r, j, live):
                    n = TPB * r + j
                    if live(HT):
                        u, slot = n - HT, (j - HT) % 4
                        act.wait_ge(s["h_t"], u + 1)
                        wait(act, s["q" if layer == 0 else "scores"], u - 3)
                        nc.scalar.copy(h_parts[:, slot, 0], ps_h[:, :, :]).then_inc(s["h_hi"], 1)
                    if layer == 0 and live(QP):
                        u, slot = n - QP, (j - QP) % 2
                        act.wait_ge(s["q"], u + 1)
                        wait(act, s["scores"], u - 1)
                        for m in range(KC):
                            last = nc.scalar.activation(q_parts[:, slot, 0, m], ps_q[:, m], ACT.Identity, bias=g.q_bias[:, m:m + 1])
                        last.then_inc(s["q_hi"], 1)
                    if live(OT):
                        u, slot = n - OT, (j - OT) % 2
                        act.wait_ge(s["o_t"], u + 1)
                        wait(act, s["projected"], u - 1)
                        nc.scalar.copy(o_parts[:, slot, 0], ps_o[:, :, :]).then_inc(s["o_hi"], 1)
                    if live(EX):
                        u, slot = n - EX, (j - EX) % 4
                        act.wait_ge(s["shifted"], u + 1)
                        nc.scalar.activation(probs[:, slot], probs[:, slot], ACT.Exp, scale=exp_scale).then_inc(s["exp"], 1)
                    if live(LN):
                        u, slot = n, j % 2
                        wait(act, s["h_t"], u - 1)
                        if since(u - 1):
                            act.sem_inc(s["held"], 1)
                        nc.scalar.activation(normed[:, slot], res[:, u, :], ACT.Identity, bias=g.shift[:, bass.ds(u, 1)],
                                             scale=g.rstd[:, bass.ds(u, 1)]).then_inc(s["normed"], 1)
                    if live(PT):
                        u, slot = n - PT, (j - PT) % 2
                        wait(act, s["av"], u - 1)
                        for half in range(2):
                            pairs = slice(PAIRS // 2 * half, PAIRS // 2 * (half + 1))
                            act.wait_ge(s["p_t"], 2 * u + half + 1)
                            nc.scalar.copy(probs_t[:, slot, pairs], ps_p[:, pairs]).then_inc(s["p_t_out"], 1)
                pipe.run(act, step)

            @block.vector
            def _(dve):
                def step(r, j, live):
                    n = TPB * r + j
                    if live(RES):
                        u = n - RES
                        dve.wait_ge(s["projected"], u + 1)
                        nc.vector.scalar_tensor_tensor(res[:, u, :], ps_y, 1.0 / WS, res[:, u, :], ALU.mult,
                                                       ALU.add).then_inc(s["residual"], 1)
                    if layer == 1 and live(LN):
                        u, slot = n, j % 4
                        dve.wait_ge(mask_loaded[slot], 16 * r + 16)
                        wait(dve, s["scores"], u - 3)
                        nc.vector.tensor_scalar(mask_fill[:, slot], mask[:, slot], 0.0, -1e20, ALU.is_equal,
                                                ALU.mult).then_inc(s["fill"], 1)
                    if live(HT):
                        u, slot = n - HT, (j - HT) % 4
                        dve.wait_ge(s["h_hi"], u + 1)
                        nc.vector.tensor_tensor(h_parts[:, slot, 1], ps_h[:, :, :], h_parts[:, slot, 0], ALU.subtract).then_inc(s["h_lo"], 1)
                    if layer == 0 and live(QP):
                        u, slot = n - QP, (j - QP) % 2
                        dve.wait_ge(s["q_hi"], u + 1)
                        for m in range(KC):
                            last = nc.vector.scalar_tensor_tensor(q_parts[:, slot, 1, m], ps_q[:, m], g.q_bias[:, m:m + 1],
                                                                  q_parts[:, slot, 0, m], ALU.add, ALU.subtract)
                        last.then_inc(s["q_lo"], 1)
                    if live(OT):
                        u, slot = n - OT, (j - OT) % 2
                        dve.wait_ge(s["o_hi"], u + 1)
                        nc.vector.tensor_tensor(o_parts[:, slot, 1], ps_o[:, :, :], o_parts[:, slot, 0], ALU.subtract).then_inc(s["o_lo"], 1)
                    if live(RES):
                        u = n - RES
                        dve.wait_ge(s["residual"], u + 1)
                        nc.vector.bn_stats(g.stats[:, u, :], res[:, u, :])
                    if layer == 0 and live(MX):
                        u, slot = n - MX, (j - MX) % 4
                        dve.wait_ge(s["filled"], u + 1)
                        nc.vector.tensor_reduce(row_max[:, slot], probs[:, slot], AX.X, ALU.max).then_inc(s["max"], 1)
                    if live(SC):
                        u, slot = n - SC, (j - SC) % 4
                        dve.wait_ge(s["scores"], u + 1)
                        wait(dve, s["p_t"], 2 * (u - 3))
                        t = probs[:, slot]
                        if layer == 0:
                            batch = r + (j - SC) // TPB
                            dve.wait_ge(mask_loaded[slot], 16 * batch + 16)
                            nc.vector.tensor_tensor(t, ps_s[:, :, :], bc(mask[:, slot], 1, HEADS), ALU.mult).then_inc(s["mask_used"], 1)
                            dve.wait_ge(s["mask_used"], u + 1)
                            wait(dve, s["filled"], u)
                            nc.vector.tensor_scalar(fill[:, :, :], t, 0.0, -1e9 / exp_scale, ALU.is_equal, ALU.mult).then_inc(s["fill"], 1)
                        else:
                            nc.vector.tensor_reduce(row_max[:, slot], ps_s[:, :, :], AX.X, ALU.max).then_inc(s["max"], 1)
                            dve.wait_ge(s["max"], u + 1)
                            nc.vector.tensor_tensor(t, ps_s[:, :, :], bc(row_max[:, slot], 2, KEYS),
                                                    ALU.subtract).then_inc(s["shifted"], 1)
                    if live(AV):
                        u, slot = n - AV, (j - AV) % 2
                        dve.wait_ge(s["av"], u + 1)
                        nc.vector.reciprocal(row_sum[:, slot], ps_v[:, :, HD]).then_inc(s["recip"], 1)
                        dve.wait_ge(s["recip"], u + 1)
                        wait(dve, s["o_t"], u - 1)
                        nc.vector.tensor_tensor(heads_out[:, slot].rearrange("p (h d) -> p h d", d=HD), ps_v[:, :, 0:HD],
                                                bc(row_sum[:, slot], 2, HD), ALU.mult).then_inc(s["heads"], 1)
                pipe.run(dve, step)


NC = B
PAIR_I = NI // 2
(M_H, M_G, M_U, M_V, M_O, S_H, INV_H, K_G, S_G, K_U, K_V, K_O, K_OUT, TMP, S_U, S_V) = range(16)


def col(g, c):
    return g.scal[:, c:c + 1]


def scale_of(chain, nc, g, peak, unit, out):
    if unit is not None:
        chain(nc.vector.tensor_scalar(col(g, TMP), col(g, peak), col(g, unit), 1.0 / QMAX, ALU.mult, ALU.mult))
    else:
        chain(nc.vector.tensor_scalar(col(g, TMP), col(g, peak), 1.0 / QMAX, None, ALU.mult))
    chain(nc.vector.tensor_scalar(col(g, out), col(g, TMP), 1e-12, None, ALU.max))


def ffn_prep(nc, g, io, w_gu, w_d, h_parts_t, scratch):
    NB = NI * D // QB
    WCOLS = NI * D
    with Stage(nc, "quant") as st:
        raw = scratch[:, 0:6 * WCOLS].bitcast(F32).rearrange("p (t n) -> p t n", t=3)
        ratio = scratch[:, 6 * WCOLS:8 * WCOLS].bitcast(F32)
        w_parts = scratch[:, 8 * WCOLS:10 * WCOLS].bitcast(F16).rearrange("p (a n) -> p a n", a=2)
        block_max = st.sb("block_max", [P, NB], F32)
        block_step = st.sb("block_step", [P, NB], F32)
        block_inv = st.sb("block_inv", [P, NB], F32)
        w_int = st.sb("w_int", [P, WCOLS], I16)
        peaks = st.sb("peaks", [P, NC], F32)
        row_peak = st.sb("row_peak", [P, 1], F32)
        h_int = st.sb("h_int", [P, 2, TPB, D], I16)
        h_split = st.sb("h_split", [P, 2, 2, TPB, D], F16)
        sems = (st.sem("stat_steps"), st.sem("var_ready"), st.sem("std_ready"), st.sem("rstd_ready"))
        s = {k: st.sem(k) for k in ("raw_loaded", "steps", "w_split", "w_t", "w_stored", "applied",
                                    "peak", "row_peak", "all_peak", "h_int", "h_hi", "h_lo", "h_t", "h_stored")}
        pipe = Tiles(NC, 2, 2, 1)
        ps16 = [g.psum[:, b, :].bitcast(F16) for b in range(8)]
        with nc.Block() as block:
            @block.sync
            def _(sp):
                for n, name in enumerate(("w_gate", "w_up")):
                    sp.dma_start(raw[:, n].rearrange("p (i d) -> p i d", d=D),
                                 io[f"L0_ffn_{name}"].rearrange("(i p) d -> p i d", p=P)).then_inc(s["raw_loaded"], 16)
                sp.dma_start(raw[:, 2].rearrange("p (r i) -> p r i", r=KC),
                             io["L0_ffn_w_down"].rearrange("(r p) i -> p r i", p=P)).then_inc(s["raw_loaded"], 16)
                sp.wait_ge(s["raw_loaded"], 48)

            @block.gpsimd
            def _(pool):
                pool.wait_ge(s["row_peak"], 1)
                nc.gpsimd.partition_all_reduce(col(g, M_H), row_peak[:, :], P, RMAX).then_inc(s["all_peak"], 1)

            @block.scalar
            def _(act):
                finish_stats(nc, act, g, "act", sems)
                act.wait_ge(sems[3], 1)
                with act.Fori(0, NC) as c:
                    for t in range(TPB):
                        u = c * TPB + t
                        last = nc.scalar.activation(g.res[:, u, :], g.res[:, u, :], ACT.Identity,
                                                    bias=g.shift[:, bass.ds(u, 1)], scale=g.rstd[:, bass.ds(u, 1)])
                    last.then_inc(s["applied"], 1)
                for n in range(12):
                    act.wait_ge(s["w_t"], n + 1)
                    src = ps16[4 + n % 4][:, 0:FF]
                    part, q = (n % 4) // 2, n % 2
                    if n < 8:
                        dst = w_gu[:, part, n // 4, q, :]
                    else:
                        dst = w_d[:, part, 3 * q:3 * q + 3, :].rearrange("p i d -> p (i d)")
                    nc.scalar.copy(dst, src).then_inc(s["w_stored"], 1)

                def step(r, j, live):
                    if live(0):
                        c = 2 * r + j
                        act.wait_ge(s["h_int"], c + 1)
                        wait(act, s["h_t"], c - 1)
                        nc.scalar.copy(h_split[:, j, 0], h_int[:, j]).then_inc(s["h_hi"], 1)
                    if live(1):
                        c, slot = 2 * r + j - 1, (j - 1) % 2
                        act.wait_ge(s["h_t"], c + 1)
                        for part in range(2):
                            last = nc.scalar.copy(h_parts_t[:, part, :, bass.ds(c * S, S)],
                                                  ps16[2 * slot + part].rearrange("p (k n) -> p k n", k=KC))
                        last.then_inc(s["h_stored"], 1)
                pipe.run(act, step)

            @block.tensor
            def _(pe):
                for t in range(3):
                    pe.wait_ge(s["w_split"], t + 1)
                    for n in range(4):
                        part, q = n // 2, n % 2
                        wait(pe, s["w_stored"], 4 * (t - 1) + n + 1)
                        for m in range(6):
                            if t < 2:
                                src = w_parts[:, part, D * m + P * q:D * m + P * (q + 1)]
                            else:
                                at = FF * (m % 2) + P * (3 * q + m // 2)
                                src = w_parts[:, part, at:at + P]
                            last = nc.tensor.transpose(ps16[4 + n][:, P * m:P * (m + 1)], src, g.ident16[:, :])
                        last.then_inc(s["w_t"], 1)

                def step(r, j, live):
                    if live(1):
                        c, slot = 2 * r + j - 1, (j - 1) % 2
                        pe.wait_ge(s["h_lo"], c + 1)
                        wait(pe, s["h_stored"], c - 1)
                        for part in range(2):
                            for k in range(KC):
                                for t in range(TPB):
                                    at = k * S + t * P
                                    last = nc.tensor.transpose(ps16[2 * slot + part][:, at:at + P],
                                                               h_split[:, slot, part, t, P * k:P * (k + 1)], g.ident16[:, :])
                        last.then_inc(s["h_t"], 1)
                pipe.run(pe, step)

            @block.vector
            def _(dve):
                finish_stats(nc, dve, g, "dve", sems)
                dve.wait_ge(sems[3], 1)
                chain = Chain(dve, s["steps"])
                dve.wait_ge(s["raw_loaded"], 48)
                for t in range(3):
                    blocks = raw[:, t].rearrange("p (b q) -> p b q", q=QB)
                    chain(nc.vector.tensor_reduce(block_max[:, :], blocks, AX.X, ALU.max, apply_absolute_value=True))
                    chain(nc.vector.tensor_scalar(block_step[:, :], block_max[:, :], 1.0 / 7.0, 1e-12, ALU.mult, ALU.max))
                    chain(nc.vector.reciprocal(block_inv[:, :], block_step[:, :]))
                    r3 = ratio.rearrange("p (b q) -> p b q", q=QB)
                    i3 = w_int[:, :].rearrange("p (b q) -> p b q", q=QB)
                    chain(nc.vector.tensor_tensor(i3, blocks, bc(block_inv[:, :], 2, QB), ALU.mult))
                    chain(nc.vector.tensor_tensor(r3, i3, bc(block_step[:, :], 2, QB), ALU.mult))
                    if t:
                        dve.wait_ge(s["w_t"], 4 * t)
                    chain(nc.vector.tensor_scalar(w_parts[:, 0], ratio, WS, None, ALU.mult))
                    nc.vector.scalar_tensor_tensor(w_parts[:, 1], ratio, WS, w_parts[:, 0], ALU.mult,
                                                   ALU.subtract).then_inc(s["w_split"], 1)
                    dve.wait_ge(s["w_split"], t + 1)
                with dve.Fori(0, NC) as c:
                    dve.wait_ge(s["applied"], c + 1)
                    nc.vector.tensor_reduce(peaks[:, bass.ds(c, 1)], g.res[:, bass.ds(c * TPB, TPB), :], AX.XY, ALU.max,
                                            apply_absolute_value=True).then_inc(s["peak"], 1)
                dve.wait_ge(s["peak"], NC)
                nc.vector.tensor_reduce(row_peak[:, :], peaks[:, :], AX.X, ALU.max).then_inc(s["row_peak"], 1)
                dve.wait_ge(s["all_peak"], 1)
                scale_of(chain, nc, g, M_H, None, S_H)
                chain(nc.vector.reciprocal(col(g, INV_H), col(g, S_H)))

                def step(r, j, live):
                    if live(0):
                        c = 2 * r + j
                        wait(dve, s["h_lo"], c - 1)
                        nc.vector.tensor_scalar(h_int[:, j], g.res[:, bass.ds(c * TPB, TPB), :], col(g, INV_H), None,
                                                ALU.mult).then_inc(s["h_int"], 1)
                        dve.wait_ge(s["h_hi"], c + 1)
                        nc.vector.tensor_tensor(h_split[:, j, 1], h_int[:, j], h_split[:, j, 0], ALU.subtract).then_inc(s["h_lo"], 1)
                pipe.run(dve, step)


def project_in(nc, pe, g, w_gu, which, i, bank, h_parts_t, c):
    for k in range(KC):
        for m, (a, b) in enumerate(PASSES):
            last = nc.tensor.matmul(g.psum[:, bank, :], w_gu[:, a, which, k, P * i:P * (i + 1)],
                                    h_parts_t[:, b, k, bass.ds(c * S, S)],
                                    start=(k == 0 and m == 0), stop=(k == KC - 1 and m == 2))
    return last


def ffn_peaks(nc, g, w_gu, h_parts_t):
    pipe = Tiles(NC, 1, 1, 0)
    SLOTS = 3
    with Stage(nc, "peaks") as st:
        peaks = st.sb("peaks", [P, 2, NC * PAIR_I], F32)
        row_peak = st.sb("row_peak", [P, 2], F32)
        s = {k: st.sem(k) for k in ("product", "peak", "row_peak", "all_peak", "steps")}
        with nc.Block() as block:
            @block.tensor
            def _(pe):
                def step(r, j, live):
                    for n in range(2 * PAIR_I):
                        wait(pe, s["peak"], 2 * PAIR_I * r + n - SLOTS + 1)
                        for e in range(2):
                            last = project_in(nc, pe, g, w_gu, n // PAIR_I, 2 * (n % PAIR_I) + e, 2 * (n % SLOTS) + e, h_parts_t, r)
                        last.then_inc(s["product"], 1)
                pipe.run(pe, step)

            @block.gpsimd
            def _(pool):
                pool.wait_ge(s["row_peak"], 1)
                nc.gpsimd.partition_all_reduce(g.scal[:, M_G:M_U + 1], row_peak[:, :], P, RMAX).then_inc(s["all_peak"], 1)

            @block.vector
            def _(dve):
                def step(r, j, live):
                    for n in range(2 * PAIR_I):
                        dve.wait_ge(s["product"], 2 * PAIR_I * r + n + 1)
                        slot = 2 * (n % SLOTS)
                        nc.vector.tensor_reduce(peaks[:, n // PAIR_I, bass.ds(r * PAIR_I + n % PAIR_I, 1)], g.psum[:, slot:slot + 2, :],
                                                AX.XY, ALU.max, apply_absolute_value=True).then_inc(s["peak"], 1)
                pipe.run(dve, step)
                dve.wait_ge(s["peak"], 2 * PAIR_I * NC)
                nc.vector.tensor_reduce(row_peak[:, :], peaks[:, :, :], AX.X, ALU.max).then_inc(s["row_peak"], 1)
                dve.wait_ge(s["all_peak"], 1)
                chain = Chain(dve, s["steps"])
                chain(nc.vector.tensor_scalar(col(g, S_H), col(g, S_H), 1.0 / WS, None, ALU.mult))
                for peak, step_, k in ((M_G, S_G, K_G), (M_U, S_U, K_U)):
                    scale_of(chain, nc, g, peak, S_H, step_)
                    chain(nc.vector.reciprocal(col(g, k), col(g, step_)))
                    chain(nc.vector.tensor_scalar(col(g, k), col(g, k), col(g, S_H), None, ALU.mult))


def ffn_gate(nc, g, w_gu, h_parts_t, gate_int):
    pipe = Tiles(NC, 1, 1, 0)
    with Stage(nc, "gate") as st:
        sig = st.sb("sig", [P, PAIR_I, 2, S], F32)
        sig_int = st.sb("sig_int", [P, PAIR_I, 2, S], U16)
        peaks = st.sb("peaks", [P, NC * PAIR_I], F32)
        row_peak = st.sb("row_peak", [P, 1], F32)
        s = {k: st.sem(k) for k in ("product", "gate_int", "held", "sig", "sig_int", "value", "peak", "row_peak", "all_peak", "steps")}
        with nc.Block() as block:
            @block.tensor
            def _(pe):
                def step(r, j, live):
                    for n in range(PAIR_I):
                        wait(pe, s["gate_int"], PAIR_I * (r - 1) + n + 1)
                        for e in range(2):
                            last = project_in(nc, pe, g, w_gu, 0, 2 * n + e, 2 * n + e, h_parts_t, r)
                        last.then_inc(s["product"], 1)
                pipe.run(pe, step)

            @block.scalar
            def _(act):
                def step(r, j, live):
                    for n in range(PAIR_I):
                        u = PAIR_I * r + n
                        act.wait_ge(s["product"], u + 1)
                        kept = gate_int(n)[:, :, bass.ds(r * S, S)]
                        nc.scalar.activation(kept, g.psum[:, 2 * n:2 * n + 2, :], ACT.Identity, scale=col(g, K_G)).then_inc(s["gate_int"], 1)
                        act.wait_ge(s["gate_int"], u + 1)
                        wait(act, s["peak"], u - PAIR_I + 1)
                        act.sem_inc(s["held"], 1)
                        nc.scalar.activation(sig[:, n], kept, ACT.Sigmoid, scale=col(g, S_G)).then_inc(s["sig"], 1)
                pipe.run(act, step)

            @block.gpsimd
            def _(pool):
                pool.wait_ge(s["row_peak"], 1)
                nc.gpsimd.partition_all_reduce(col(g, M_V), row_peak[:, :], P, RMAX).then_inc(s["all_peak"], 1)

            @block.vector
            def _(dve):
                def peak_of(r, n):
                    dve.wait_ge(s["sig_int"], PAIR_I * r + n + 1)
                    nc.vector.tensor_tensor(sig[:, n], gate_int(n)[:, :, bass.ds(r * S, S)], sig_int[:, n],
                                            ALU.mult).then_inc(s["value"], 1)
                    dve.wait_ge(s["value"], PAIR_I * r + n + 1)
                    nc.vector.tensor_reduce(peaks[:, bass.ds(r * PAIR_I + n, 1)], sig[:, n], AX.XY, ALU.max,
                                            apply_absolute_value=True).then_inc(s["peak"], 1)

                def step(r, j, live):
                    for n in range(PAIR_I):
                        u = PAIR_I * r + n
                        dve.wait_ge(s["sig"], u + 1)
                        wait(dve, s["value"], u - PAIR_I + 1)
                        nc.vector.tensor_scalar(sig_int[:, n], sig[:, n], 65536.0, 65535.0, ALU.mult, ALU.min).then_inc(s["sig_int"], 1)
                        peak_of(r, n)
                pipe.run(dve, step)
                dve.wait_ge(s["peak"], PAIR_I * NC)
                nc.vector.tensor_reduce(row_peak[:, :], peaks[:, :], AX.X, ALU.max).then_inc(s["row_peak"], 1)
                dve.wait_ge(s["all_peak"], 1)
                chain = Chain(dve, s["steps"])
                chain(nc.vector.tensor_scalar(col(g, S_G), col(g, S_G), 1.0 / 65536.0, None, ALU.mult))
                scale_of(chain, nc, g, M_V, S_G, S_V)
                chain(nc.vector.reciprocal(col(g, K_V), col(g, S_V)))
                chain(nc.vector.tensor_scalar(col(g, K_V), col(g, K_V), col(g, S_G), None, ALU.mult))
                chain(nc.vector.tensor_scalar(col(g, S_G), col(g, S_G), 65536.0, None, ALU.mult))


def ffn_up(nc, g, io, w_gu, h_parts_t, gate_int):
    pipe = Tiles(NC, 1, 1, 0)
    with Stage(nc, "up") as st:
        up_int = st.sb("up_int", [P, PAIR_I, 2, S], I16)
        sig = st.sb("sig", [P, PAIR_I, 2, S], F32)
        sig_int = st.sb("sig_int", [P, 2, S], U16)
        peaks = st.sb("peaks", [P, NC * PAIR_I], F32)
        row_peak = st.sb("row_peak", [P, 1], F32)
        stored = [st.sem(f"up_stored{n}") for n in range(PAIR_I)]
        s = {k: st.sem(k) for k in ("product", "up_int", "sig", "sig_int", "gate_int", "value", "peak", "row_peak",
                                    "all_peak", "steps")}
        with nc.Block() as block:
            @block.sync
            def _(sp):
                with sp.Fori(0, NC) as c:
                    for n in range(PAIR_I):
                        sp.wait_ge(s["up_int"], c * PAIR_I + n + 1)
                        sp.dma_start(io["up_spill"][:, c, n], up_int[:, n]).then_inc(stored[n], 16)
                for n in range(PAIR_I):
                    sp.wait_ge(stored[n], 16 * NC)

            @block.tensor
            def _(pe):
                def step(r, j, live):
                    for n in range(PAIR_I):
                        wait(pe, s["up_int"], PAIR_I * (r - 1) + n + 1)
                        for e in range(2):
                            last = project_in(nc, pe, g, w_gu, 1, 2 * n + e, 2 * n + e, h_parts_t, r)
                        last.then_inc(s["product"], 1)
                pipe.run(pe, step)

            @block.scalar
            def _(act):
                def step(r, j, live):
                    for n in range(PAIR_I):
                        u = PAIR_I * r + n
                        wait(act, s["peak"], u - PAIR_I + 1)
                        nc.scalar.activation(sig[:, n], gate_int(n)[:, :, bass.ds(r * S, S)], ACT.Sigmoid,
                                             scale=col(g, S_G)).then_inc(s["sig"], 1)
                        act.wait_ge(s["product"], u + 1)
                        wait(act, s["value"], u - PAIR_I + 1)
                        wait(act, stored[n], 16 * r)
                        nc.scalar.activation(up_int[:, n], g.psum[:, 2 * n:2 * n + 2, :], ACT.Identity,
                                             scale=col(g, K_U)).then_inc(s["up_int"], 1)
                pipe.run(act, step)

            @block.gpsimd
            def _(pool):
                pool.wait_ge(s["row_peak"], 1)
                nc.gpsimd.partition_all_reduce(col(g, M_O), row_peak[:, :], P, RMAX).then_inc(s["all_peak"], 1)

            @block.vector
            def _(dve):
                def step(r, j, live):
                    for n in range(PAIR_I):
                        u = PAIR_I * r + n
                        kept = gate_int(n)[:, :, bass.ds(r * S, S)]
                        dve.wait_ge(s["sig"], u + 1)
                        wait(dve, s["gate_int"], u)
                        nc.vector.tensor_scalar(sig_int[:, :, :], sig[:, n], 65536.0, 65535.0, ALU.mult, ALU.min).then_inc(s["sig_int"], 1)
                        dve.wait_ge(s["sig_int"], u + 1)
                        nc.vector.scalar_tensor_tensor(kept, kept, col(g, K_V), sig_int[:, :, :], ALU.mult, ALU.mult).then_inc(s["gate_int"], 1)
                        dve.wait_ge(s["gate_int"], u + 1)
                        dve.wait_ge(s["up_int"], u + 1)
                        nc.vector.tensor_tensor(sig[:, n], kept, up_int[:, n], ALU.mult).then_inc(s["value"], 1)
                        dve.wait_ge(s["value"], u + 1)
                        nc.vector.tensor_reduce(peaks[:, bass.ds(r * PAIR_I + n, 1)], sig[:, n], AX.XY, ALU.max,
                                                apply_absolute_value=True).then_inc(s["peak"], 1)
                pipe.run(dve, step)
                dve.wait_ge(s["peak"], PAIR_I * NC)
                nc.vector.tensor_reduce(row_peak[:, :], peaks[:, :], AX.X, ALU.max).then_inc(s["row_peak"], 1)
                dve.wait_ge(s["all_peak"], 1)
                chain = Chain(dve, s["steps"])
                chain(nc.vector.tensor_scalar(col(g, S_V), col(g, S_V), col(g, S_U), None, ALU.mult))
                scale_of(chain, nc, g, M_O, S_V, K_OUT)
                chain(nc.vector.reciprocal(col(g, K_O), col(g, K_OUT)))
                chain(nc.vector.tensor_scalar(col(g, K_O), col(g, K_O), col(g, S_V), None, ALU.mult))
                chain(nc.vector.tensor_scalar(col(g, K_OUT), col(g, K_OUT), 1.0 / WS, None, ALU.mult))


def ffn_down(nc, g, io, w_d, gate_int, res):
    pipe = Tiles(NC, 2, 2, 0)
    with Stage(nc, "down") as st:
        up_int = st.sb("up_int", [P, PAIR_I, 2, S], I16)
        o_int = st.sb("o_int", [P, PAIR_I, 2, S], I16)
        o_parts = st.sb("o_parts", [P, PAIR_I, 2, 2, S], F16)
        x1 = st.sb("x1", [P, 2, TPB, D], F32)
        up_loaded = [st.sem(f"up_loaded{n}") for n in range(PAIR_I)]
        x1_loaded = [st.sem(f"x1_loaded{n}") for n in range(2)]
        s = {k: st.sem(k) for k in ("o_int", "o_hi", "o_lo", "used", "sum", "residual")}
        with nc.Block() as block:
            @block.sync
            def _(sp):
                def step(r, j, live):
                    c = 2 * r + j
                    for n in range(PAIR_I):
                        wait(sp, s["o_int"], PAIR_I * (c - 1) + n + 1)
                        sp.dma_start(up_int[:, n], io["up_spill"][:, c, n]).then_inc(up_loaded[n], 16)
                    wait(sp, s["residual"], c - 1)
                    sp.dma_start(x1[:, j], io["x1_spill"][:, c]).then_inc(x1_loaded[j], 16)
                pipe.run(sp, step)

            @block.tensor
            def _(pe):
                def step(r, j, live):
                    c = 2 * r + j
                    wait(pe, s["residual"], c - 1)
                    for n in range(PAIR_I):
                        pe.wait_ge(s["o_lo"], PAIR_I * c + n + 1)
                        for e in range(2):
                            for t in range(TPB):
                                for m, (a, b) in enumerate(PASSES):
                                    last = nc.tensor.matmul(g.psum[:, TPB * j + t, 0:D], o_parts[:, n, a, e, P * t:P * (t + 1)],
                                                            w_d[:, b, 2 * n + e, :], start=(n == 0 and e == 0 and m == 0),
                                                            stop=(n == PAIR_I - 1 and e == 1 and m == 2))
                        last.then_inc(s["used"], 1)
                pipe.run(pe, step)

            @block.scalar
            def _(act):
                def step(r, j, live):
                    c = 2 * r + j
                    for n in range(PAIR_I):
                        u = PAIR_I * c + n
                        act.wait_ge(s["o_int"], u + 1)
                        wait(act, s["used"], u - PAIR_I + 1)
                        nc.scalar.copy(o_parts[:, n, 0], o_int[:, n]).then_inc(s["o_hi"], 1)
                pipe.run(act, step)

            @block.vector
            def _(dve):
                def lows(u, n):
                    dve.wait_ge(s["o_hi"], u + 1)
                    nc.vector.tensor_tensor(o_parts[:, n, 1], o_int[:, n], o_parts[:, n, 0], ALU.subtract).then_inc(s["o_lo"], 1)

                def step(r, j, live):
                    c = 2 * r + j
                    for n in range(PAIR_I):
                        u = PAIR_I * c + n
                        dve.wait_ge(up_loaded[n], 16 * c + 16)
                        wait(dve, s["o_lo"], u - PAIR_I + 1)
                        nc.vector.scalar_tensor_tensor(o_int[:, n], gate_int(n)[:, :, bass.ds(c * S, S)], col(g, K_O), up_int[:, n],
                                                       ALU.mult, ALU.mult).then_inc(s["o_int"], 1)
                        if n:
                            lows(u - 1, n - 1)
                    lows(PAIR_I * c + PAIR_I - 1, PAIR_I - 1)
                    if not (isinstance(c, int) and c == 0):
                        residual(r if j else r - 1, 1 - j)

                def residual(r, j):
                    c = 2 * r + j
                    dve.wait_ge(s["used"], PAIR_I * c + PAIR_I)
                    dve.wait_ge(x1_loaded[j], 16 * r + 16)
                    for t in range(TPB):
                        nc.vector.scalar_tensor_tensor(res[:, c * TPB + t, :], g.psum[:, TPB * j + t, 0:D], col(g, K_OUT), x1[:, j, t],
                                                       ALU.mult, ALU.add).then_inc(s["sum"], 1)
                    for t in range(TPB):
                        dve.wait_ge(s["sum"], TPB * c + t + 1)
                        last = nc.vector.bn_stats(g.stats[:, c * TPB + t, :], res[:, c * TPB + t, :])
                    last.then_inc(s["residual"], 1)
                pipe.run(dve, step)
                residual(NC // 2 - 1, 1)


def moe_prep(nc, g, io, res, h_t):
    LN, _, HT, LO, LG = range(5)
    ABSENT = -3e38
    pad = NE + TOP_K
    pipe = Tiles(NT, 4, 8, LG)
    with Stage(nc, "route") as st:
        normed = st.sb("normed", [P, 4, D], F32)
        gate_raw = st.sb("gate_raw", [P, KC, NE], F32)
        gate_parts = st.sb("gate_parts", [P, 2, KC, NE], F16)
        e_bias = st.sb("e_bias", [P, NE], F32)
        scores = st.sb("scores", [P, NT, NE], F32)
        padded = st.sb("padded", [P, NT, pad], F32)
        left = st.sb("left", [P, NT, pad], F32)
        best = st.sb("best", [P, NT, 8], F32)
        wins = st.sb("wins", [P, NT, GROUPS], F32)
        high = st.sb("high", [P, NT, GROUPS, 2], F32)
        low = st.sb("low", [P, NT, GROUPS, 2], F32)
        group_sum = st.sb("group_sum", [P, NT, GROUPS], F32)
        second = st.sb("second", [P, NT, GROUPS], F32)
        group_rank = st.sb("group_rank", [P, NT, GROUPS], F32)
        total = st.sb("total", [P, NT], F32)
        choice = padded[:, :, 0:NE]
        sems = (st.sem("stat_steps"), st.sem("var_ready"), st.sem("std_ready"), st.sem("rstd_ready"))
        s = {k: st.sem(k) for k in ("loaded", "gate_hi", "gate_lo", "normed", "h_t", "h_hi", "h_lo", "logits",
                                    "logits_out", "padded", "scores", "steps", "held")}
        with nc.Block() as block:
            @block.sync
            def _(sp):
                sp.dma_start(gate_raw[:, :, :], io["moe_gate_T"].rearrange("(k p) e -> p k e", p=P)).then_inc(s["loaded"], 16)
                sp.dma_start(e_bias[:, :], io["moe_e_bias"].rearrange("(a n) -> a n", a=1).to_broadcast([P, NE])).then_inc(s["loaded"], 16)
                sp.wait_ge(s["loaded"], 32)

            @block.gpsimd
            def _(pool):
                nc.gpsimd.memset(padded[:, :, NE:], ABSENT).then_inc(s["padded"], 1)

            @block.tensor
            def _(pe):
                def step(r, j, live):
                    n = 4 * r + j
                    if live(HT):
                        u, slot = n - HT, (j - HT) % 4
                        pe.wait_ge(s["normed"], u + 1)
                        wait(pe, s["h_lo"], u - 3)
                        for k in range(KC):
                            last = nc.tensor.transpose(g.psum[:, slot, P * k:P * (k + 1)], normed[:, slot, P * k:P * (k + 1)], g.ident32[:, :])
                        last.then_inc(s["h_t"], 1)
                    if live(LG):
                        u, slot = n - LG, (j - LG) % 4
                        pe.wait_ge(s["h_lo"], u + 1)
                        wait(pe, s["logits_out"], u - 3)
                        if isinstance(u, int) and u == 0:
                            pe.wait_ge(s["gate_lo"], 1)
                        for k in range(KC):
                            for i, (a, b) in enumerate(PASSES):
                                last = nc.tensor.matmul(g.psum[:, 4 + slot, 0:NE], h_t[:, a, k, bass.ds(u * P, P)], gate_parts[:, b, k],
                                                        start=(k == 0 and i == 0), stop=(k == KC - 1 and i == 2))
                        last.then_inc(s["logits"], 1)
                pipe.run(pe, step)

            @block.scalar
            def _(act):
                finish_stats(nc, act, g, "act", sems)
                act.wait_ge(sems[3], 1)
                act.wait_ge(s["loaded"], 32)
                nc.scalar.mul(gate_parts[:, 0], gate_raw[:, :, :], WS).then_inc(s["gate_hi"], 1)

                def step(r, j, live):
                    n = 4 * r + j
                    if live(HT):
                        u, slot = n - HT, (j - HT) % 4
                        act.wait_ge(s["h_t"], u + 1)
                        nc.scalar.copy(h_t[:, 0, :, bass.ds(u * P, P)],
                                       g.psum[:, slot, 0:D].rearrange("p (k n) -> p k n", k=KC)).then_inc(s["h_hi"], 1)
                    if live(LN):
                        wait(act, s["h_t"], n - 3)
                        if since(n - 3):
                            act.sem_inc(s["held"], 1)
                        nc.scalar.activation(normed[:, j], res[:, n, :], ACT.Identity, bias=g.shift[:, bass.ds(n, 1)],
                                             scale=g.rstd[:, bass.ds(n, 1)]).then_inc(s["normed"], 1)
                    if live(LG):
                        u, slot = n - LG, (j - LG) % 4
                        act.wait_ge(s["logits"], u + 1)
                        nc.scalar.activation(scores[:, u, :], g.psum[:, 4 + slot, 0:NE], ACT.Sigmoid, scale=1.0 / WS).then_inc(s["logits_out"], 1)
                pipe.run(act, step)

            @block.vector
            def _(dve):
                finish_stats(nc, dve, g, "dve", sems)
                dve.wait_ge(sems[3], 1)
                dve.wait_ge(s["gate_hi"], 1)
                nc.vector.scalar_tensor_tensor(gate_parts[:, 1], gate_raw[:, :, :], WS, gate_parts[:, 0], ALU.mult,
                                               ALU.subtract).then_inc(s["gate_lo"], 1)

                def step(r, j, live):
                    n = 4 * r + j
                    if live(LO):
                        u, slot = n - LO, (j - LO) % 4
                        dve.wait_ge(s["h_hi"], u + 1)
                        nc.vector.tensor_tensor(h_t[:, 1, :, bass.ds(u * P, P)], g.psum[:, slot, 0:D].rearrange("p (k n) -> p k n", k=KC),
                                                h_t[:, 0, :, bass.ds(u * P, P)], ALU.subtract).then_inc(s["h_lo"], 1)
                pipe.run(dve, step)

                nc.vector.memset(g.expert_w[:, 0:1, :], 1.0 / WS)
                dve.wait_ge(s["logits_out"], NT)
                chain = Chain(dve, s["steps"])
                tt = nc.vector.tensor_tensor
                chain(tt(choice, scores[:, :, :], bc(e_bias[:, :], 1, NT), ALU.add))
                quads = choice.rearrange("p t (g a b) -> p t g a b", a=2, b=2)
                chain(tt(high[:, :, :, :], quads[:, :, :, :, 0], quads[:, :, :, :, 1], ALU.max))
                chain(tt(low[:, :, :, :], quads[:, :, :, :, 0], quads[:, :, :, :, 1], ALU.min))
                sums, seconds = group_sum[:, :, :], second[:, :, :]
                chain(tt(sums, high[:, :, :, 0], high[:, :, :, 1], ALU.min))
                chain(tt(seconds, low[:, :, :, 0], low[:, :, :, 1], ALU.max))
                chain(tt(seconds, seconds, sums, ALU.max))
                chain(tt(sums, high[:, :, :, 0], high[:, :, :, 1], ALU.max))
                chain(tt(sums, sums, seconds, ALU.add))
                chain(nc.vector.memset(group_rank[:, :, :], 0.0))
                for n in range(GROUPS):
                    one = group_sum[:, :, n:n + 1]
                    chain(nc.vector.memset(wins[:, :, n:n + 1], 0.0))
                    if n + 1 < GROUPS:
                        chain(tt(wins[:, :, n + 1:], one.to_broadcast([P, NT, GROUPS - 1 - n]), group_sum[:, :, n + 1:], ALU.is_ge))
                    if n:
                        chain(tt(wins[:, :, 0:n], one.to_broadcast([P, NT, n]), group_sum[:, :, 0:n], ALU.is_gt))
                    chain(tt(group_rank[:, :, :], group_rank[:, :, :], wins[:, :, :], ALU.add))
                chain(nc.vector.tensor_scalar(group_rank[:, :, :], group_rank[:, :, :], float(TOPK_GROUP), None, ALU.is_lt))
                by_group = choice.rearrange("p t (g a) -> p t g a", g=GROUPS)
                chain(tt(by_group, by_group, bc(group_rank[:, :, :], 3, PER_GROUP), ALU.mult))
                for t in range(NT):
                    last = nc.vector.max(best[:, t, :], choice[:, t, :])
                chain(last)
                chain(nc.vector.memset(best[:, :, TOP_K:], ABSENT))
                dve.wait_ge(s["padded"], 1)
                for t in range(NT):
                    last = nc.vector.match_replace(left[:, t, :], best[:, t, :], padded[:, t, :], ABSENT)
                chain(last)
                chain(tt(left[:, :, 0:NE], left[:, :, 0:NE], choice, ALU.not_equal))
                chain(tt(scores[:, :, :], scores[:, :, :], left[:, :, 0:NE], ALU.mult))
                chain(nc.vector.tensor_reduce(total[:, :], scores[:, :, :], AX.X, ALU.add))
                chain(nc.vector.tensor_scalar(total[:, :], total[:, :], 1e-20, None, ALU.add))
                chain(nc.vector.reciprocal(total[:, :], total[:, :]))
                chain(nc.vector.tensor_scalar(total[:, :], total[:, :], SCALING / WS, None, ALU.mult))
                tt(g.expert_w[:, 1:, :], scores[:, :, :].rearrange("p t e -> p e t"), bc(total[:, :], 1, NE), ALU.mult)


def moe(nc, g, io, res, h_t):
    WN = 2 * KC * INTER + D
    HALF = 2
    with Stage(nc, "moe") as st:
        raw = st.sb("raw", [P, 2, WN], F32)
        w = st.sb("w", [P, 2, 2, WN], F16)
        gated = st.sb("gated", [P, 2, S], F32)
        inner = st.sb("inner", [P, 2, S], F32)
        parts = st.sb("parts", [P, 2, 2, S], F16)
        raw_loaded = [st.sem(f"raw_loaded{n}") for n in range(2)]
        out_stored = st.sem("out_stored")
        s = {k: st.sem(k) for k in ("w_hi", "w_lo", "gate_up", "gated", "inner", "hi", "lo", "down", "summed")}

        def sweep(eng, chunk_step):
            def expert(x, slot):
                for j in range(HALF):
                    chunk_step(x, slot, 0, j)
                with eng.Fori(1, NC // HALF) as r:
                    for j in range(HALF):
                        chunk_step(x, slot, r, j)
            expert(0, 1)
            with eng.Fori(0, NE // 2 - 1) as pair:
                for e in range(2):
                    expert(pair * 2 + e + 1, e)
            for e in range(2):
                expert(NE - 1 + e, e)

        def static(x):
            return isinstance(x, int)

        with nc.Block() as block:
            @block.sync
            def _(sp):
                sp.dma_start(raw[:, 1], io["expert_cols"][0]).then_inc(raw_loaded[1], 16)
                sp.dma_start(raw[:, 0], io["expert_cols"][1]).then_inc(raw_loaded[0], 16)
                with sp.Fori(1, NE // 2) as pair:
                    for e in range(2):
                        x = pair * 2 + e
                        sp.wait_ge(s["w_lo"], x - 1)
                        sp.dma_start(raw[:, 1 - e], io["expert_cols"][x]).then_inc(raw_loaded[1 - e], 16)
                sp.wait_ge(s["w_lo"], NE - 1)
                sp.dma_start(raw[:, 1], io["expert_cols"][NE]).then_inc(raw_loaded[1], 16)
                with sp.Fori(0, NC) as c:
                    sp.wait_ge(s["summed"], (NC * NE + c + 1) * 2)
                    sp.dma_start(io["out"][c].rearrange("(t p) d -> p t d", p=P), res[:, bass.ds(c * TPB, TPB), :]).then_inc(out_stored, 16)
                sp.wait_ge(out_stored, 16 * NC)

            @block.tensor
            def _(pe):
                def down(u, slot, j):
                    pe.wait_ge(s["lo"], u + 1)
                    wait(pe, s["summed"], (u - 1) * 2)
                    for t in range(TPB):
                        bank = g.psum[:, 4 + 2 * j + t // 2, D * (t % 2):D * (t % 2 + 1)]
                        for i, (a, b) in enumerate(PASSES):
                            last = nc.tensor.matmul(bank, parts[:, j, a, P * t:P * (t + 1)], w[:, slot, b, 2 * KC * INTER:],
                                                    start=(i == 0), stop=(i == 2))
                        if t % 2:
                            last.then_inc(s["down"], 1)

                def chunk_step(x, slot, r, j):
                    u = NC * x + HALF * r + j
                    first = static(r) and j == 0
                    if first:
                        pe.wait_ge(s["w_lo"], x + 1)
                    wait(pe, s["inner"], u - 1)
                    for q in range(2):
                        for k in range(KC):
                            at = INTER * (KC * q + k)
                            for i, (a, b) in enumerate(PASSES):
                                last = nc.tensor.matmul(g.psum[:, 2 * j + q, :], w[:, slot, a, at:at + INTER],
                                                        h_t[:, b, k, bass.ds((HALF * r + j) * S, S)],
                                                        start=(k == 0 and i == 0), stop=(k == KC - 1 and i == 2))
                    last.then_inc(s["gate_up"], 1)
                    if not (first and static(x) and x == 0):
                        down(u - 1, 1 - slot if first else slot, 1 - j)
                sweep(pe, chunk_step)
                down(NC * (NE + 1) - 1, 1, 1)

            @block.scalar
            def _(act):
                def split(x, slot):
                    act.wait_ge(raw_loaded[slot], (x - (1 - slot)) * 8 + 16)
                    wait(act, s["down"], NC * (x - 1) * 2)
                    nc.scalar.mul(w[:, slot, 0], raw[:, slot], WS).then_inc(s["w_hi"], 1)
                split(0, 1)

                def chunk_step(x, slot, r, j):
                    u = NC * x + HALF * r + j
                    act.wait_ge(s["gate_up"], u + 1)
                    wait(act, s["inner"], u - 1)
                    nc.scalar.activation(gated[:, j], g.psum[:, 2 * j, :], ACT.Silu, scale=1.0 / WS).then_inc(s["gated"], 1)
                    act.wait_ge(s["inner"], u + 1)
                    wait(act, s["down"], 2 * (u - 1))
                    nc.scalar.copy(parts[:, j, 0], inner[:, j]).then_inc(s["hi"], 1)
                    if static(r) and j == 1 and not (static(x) and x == NE):
                        split(x + 1, 1 - slot)
                sweep(act, chunk_step)

            @block.vector
            def _(dve):
                def split(x, slot):
                    dve.wait_ge(s["w_hi"], x + 1)
                    nc.vector.scalar_tensor_tensor(w[:, slot, 1], raw[:, slot], WS, w[:, slot, 0], ALU.mult,
                                                   ALU.subtract).then_inc(s["w_lo"], 1)
                split(0, 1)

                def gather(x, u, c, j):
                    if not (static(x) and x == 0):
                        dve.wait_ge(s["summed"], 2 * (u - NC + 1))
                    for t in range(TPB):
                        if t % 2 == 0:
                            dve.wait_ge(s["down"], 2 * u + t // 2 + 1)
                        tile = c * TPB + t
                        weight = g.expert_w[:, x, bass.ds(tile, 1)]
                        last = nc.vector.scalar_tensor_tensor(res[:, tile, :], g.psum[:, 4 + 2 * j + t // 2, D * (t % 2):D * (t % 2 + 1)],
                                                              weight, res[:, tile, :], ALU.mult, ALU.add)
                        if t % 2:
                            last.then_inc(s["summed"], 1)

                def chunk_step(x, slot, r, j):
                    u = NC * x + HALF * r + j
                    dve.wait_ge(s["gated"], u + 1)
                    wait(dve, s["lo"], u - 1)
                    nc.vector.scalar_tensor_tensor(inner[:, j], g.psum[:, 2 * j + 1, :], 1.0 / WS, gated[:, j], ALU.mult,
                                                   ALU.mult).then_inc(s["inner"], 1)
                    dve.wait_ge(s["inner"], u + 1)
                    dve.wait_ge(s["hi"], u + 1)
                    nc.vector.tensor_tensor(parts[:, j, 1], inner[:, j], parts[:, j, 0], ALU.subtract).then_inc(s["lo"], 1)
                    if not (static(r) and j == 0):
                        gather(x, u - 1, HALF * r + j - 1, 1 - j)
                    elif not (static(x) and x == 0):
                        gather(x - 1, u - 1, NC - 1, 1 - j)
                    if static(r) and j == 1 and not (static(x) and x == NE):
                        split(x + 1, 1 - slot)
                sweep(dve, chunk_step)
                gather(NE, NC * (NE + 1) - 1, NC - 1, 1)


class Shared:
    pass


def build(nc, io, upto=99):
    Stage.cleared = []
    with ExitStack() as ctx:
        def sb(name, shape, dt):
            return ctx.enter_context(nc.sbuf_tensor(name, shape, dt))
        g = Shared()
        g.psum = ctx.enter_context(nc.psum_tensor("psum", [P, 8, 512], F32))
        g.ident32 = sb("ident32", [P, P], F32)
        g.ident16 = sb("ident16", [P, P], F16)
        g.identb = sb("identb", [P, P], BF16)
        g.head_mask = sb("head_mask", [P, HPP, KEYS], F16)
        g.stats = sb("stats", [P, NT, 6], F32)
        g.mean = sb("mean", [P, NT], F32)
        g.var = sb("var", [P, NT], F32)
        g.rstd = sb("rstd", [P, NT], F32)
        g.shift = sb("shift", [P, NT], F32)
        g.ones_rows = sb("ones_rows", [32, P], F16)
        g.bias_rows = sb("bias_rows", [32, D], F16)
        g.q_bias = sb("q_bias", [P, KC], F32)
        wq = sb("wq", [P, 2, KC, D], F16)
        wo = sb("wo", [P, 2, KC, D], F16)
        g.scal = sb("scal", [P, 16], F32)
        g.res = sb("res", [P, NT, D], F32)
        wide = sb("wide", [P, NT * 2 * KC * P], F16)
        constants(nc, g)
        wide_rows = wide[:, :].bitcast(F32).rearrange("p (t d) -> p t d", d=D)
        res_words = g.res[:, :, :].rearrange("p t d -> p (t d)")
        shape = dict(a=2, b=B, m=KC, h=HPP)

        def attend(layer, res, kbd):
            with nc.sbuf_tensor(f"values{layer}", [P, B, PAIRS, 2 * VC], F32) as vbd:
                attention_prep(nc, g, io, layer, kbd, vbd, wq, wo)
                attention(nc, g, io, layer, res, kbd.rearrange("p a b m h k -> p a b m (h k)"), vbd, wq, wo)

        attend(0, g.res, wide[:, :].rearrange("p (a b m h k) -> p a b m h k", **shape))
        h_parts_t = wide[:, :].rearrange("p (a k n) -> p a k n", a=2, k=KC)
        with Stage(nc, "ffn") as st:
            w_d = st.sb("w_d", [P, 2, NI, D], F16)
            tail = st.sb("gate_tail", [P, 2, B * S], I16)
            front = res_words.bitcast(I16).rearrange("p (i n) -> p i n", i=NI - 2)

            def gate_int(n):
                return front[:, 2 * n:2 * n + 2, :] if n < PAIR_I - 1 else tail[:, :, :]
            with nc.sbuf_tensor("w_gu", [P, 2, 2, KC, FF], F16) as w_gu:
                ffn_prep(nc, g, io, w_gu, w_d, h_parts_t, tail[:, :, :].rearrange("p i n -> p (i n)"))
                ffn_peaks(nc, g, w_gu, h_parts_t)
                ffn_gate(nc, g, w_gu, h_parts_t, gate_int)
                ffn_up(nc, g, io, w_gu, h_parts_t, gate_int)
            ffn_down(nc, g, io, w_d, gate_int, wide_rows)
        if upto == 2:
            return dump(nc, io, wide_rows)
        attend(1, wide_rows, res_words.bitcast(F16).rearrange("p (a b m h k) -> p a b m h k", **shape))
        if upto == 3:
            return dump(nc, io, wide_rows)
        with nc.sbuf_tensor("expert_w", [P, NE + 1, NT], F32) as g.expert_w:
            h_t = res_words.bitcast(F16).rearrange("p (a k n) -> p a k n", a=2, k=KC)
            moe_prep(nc, g, io, wide_rows, h_t)
            moe(nc, g, io, wide_rows, h_t)


def dump(nc, io, rows):
    with nc.semaphore("dumped") as sem, nc.Block() as block:
        @block.sync
        def _(sp):
            sp.dma_start(io["dbg"], rows).then_inc(sem, 16)
            sp.wait_ge(sem, 16)


def arrays_of(inputs):
    import numpy as np
    a = {k: np.asarray(v) for k, v in inputs.items()}
    ctx = a["ctx_1024"]
    out = {
        "x": a["x"], "ctx": ctx, "ctx_T": ctx.transpose(2, 0, 1).reshape(D, B * KEYS),
        "mask0": a["mask_Bx1xSxS2_fk0"].reshape(B * S, KEYS), "mask1": a["mask_Bx1xSxS2_ik1"].reshape(B * S, KEYS),
        "L1_xattn_WoT": a["L1_xattn_Wo"].T,
    }
    for k in ("Wq", "bq", "Wk", "bk", "Wv", "bv", "Wo", "bo"):
        out[f"L0_xattn_{k}"] = a[f"L0_xattn_{k}"]
    for k in ("w_gate", "w_up", "w_down"):
        out[f"L0_ffn_{k}"] = a[f"L0_ffn_{k}"]
    gates = np.concatenate([a["L1_ffn_shared_gate_w"][None], a["L1_ffn_gate_proj"]])
    ups = np.concatenate([a["L1_ffn_shared_up_w"][None], a["L1_ffn_up_proj"]])
    downs = np.concatenate([a["L1_ffn_shared_down_w"][None], a["L1_ffn_down_proj"]])
    ins = np.stack([gates, ups], 1).reshape(NE + 1, 2, INTER, KC, P).transpose(0, 4, 1, 3, 2)
    out["expert_cols"] = np.concatenate([ins.reshape(NE + 1, P, 2 * KC * INTER), downs.transpose(0, 2, 1)], 2)
    out["moe_gate_T"] = a["L1_ffn_gate_w"].T
    out["moe_e_bias"] = a["L1_ffn_e_bias"]
    out["L1_xattn_bo"] = a["L1_xattn_bo"]
    return {k: np.ascontiguousarray(v) for k, v in out.items()}


def program(nc, arrays, upto=99):
    io = {k: nc.dram_tensor(k, v.shape, mybir.dt.from_np(v.dtype), kind="ExternalInput").ap() for k, v in arrays.items()}
    io["x1_spill"] = nc.dram_tensor("x1_spill", (P, B, TPB, D), F32, kind="Internal").ap()
    io["up_spill"] = nc.dram_tensor("up_spill", (P, NC, PAIR_I, 2, S), I16, kind="Internal").ap()
    if upto != 99:
        io["dbg"] = nc.dram_tensor("dbg", (P, NT, D), F32, kind="ExternalOutput").ap()
    io["out"] = nc.dram_tensor("out", (B, S, D), F32, kind="ExternalOutput").ap()
    build(nc, io, upto)


def kernel(**inputs):
    import concourse.bacc as bacc
    from concourse.bass_utils import run_bass_kernel_spmd as run
    nc = bacc.Bacc("TRN2", target_bir_lowering=False, num_devices=1)
    arrays = arrays_of(inputs)
    program(nc, arrays)
    return run(nc, [arrays], core_ids=[0]).results[0]["out"]
```
